# Optimizing a Trainium2 kernel written in Bass

```python
import numpy as np
import jax
import jax.numpy as jnp

def _softmax(x, axis=-1):
    return jax.nn.softmax(x, axis=axis)

def _gelu(x):
    return jax.nn.gelu(x, approximate=True)

def _silu(x):
    return jax.nn.silu(x)

def _sigmoid(x):
    return jax.nn.sigmoid(x)

def _layernorm(x, axis=-1, eps=1e-05):
    m = jnp.mean(x, axis=axis, keepdims=True)
    v = jnp.var(x, axis=axis, keepdims=True)
    return (x - m) / jnp.sqrt(v + eps)

def _scatter_add(tgt, idx, src, axis=0):
    return tgt.at[idx].add(src)

def _segment_sum(src, seg, n):
    return jax.ops.segment_sum(src, seg, n)
kernel_name = 'mk_gnn_ffn_d1_gnn_r32_2bf8f6'

def setup_inputs(seed: int=0):
    np.random.seed(seed)
    _w = jnp.asarray

    def _rec_inputs():
        import jax
        import jax.numpy as jnp
        _gk = jax.random.key(seed)
        x = -0.000364 + 1 * jax.random.normal(jax.random.fold_in(_gk, 1), (50000, 768), jnp.float32)
        src = jax.random.randint(jax.random.fold_in(_gk, 2), (25000,), 0, 50000, jnp.int32)
        dst = jnp.minimum((50000 * jax.random.uniform(jax.random.fold_in(_gk, 3), (25000,)) ** 2.0).astype(jnp.int32), 49999)
        _o = jnp.argsort(dst, stable=True)
        src = src[_o]
        dst = dst[_o]
        return (x, src, dst)
    x, src, dst = _rec_inputs()

    def _L0_gnn_setup():
        import jax, jax.numpy as jnp
        import numpy as np
        N = 625
        DEG = 16
        E = N * DEG
        H = 12
        DIN = 64
        DOUT = 64
        NEG_SLOPE = 0.2
        key = jax.random.key(seed)
        k_h, k_src, k_w, k_al, k_ar, k_wr = jax.random.split(key, 6)
        std = 1.414 * np.sqrt(2.0 / (DIN + DOUT))
        h = jax.random.normal(k_h, (N, H * DIN), dtype=jnp.float32)
        src = jax.random.randint(k_src, (E,), 0, N, dtype=jnp.int64)
        dst = jnp.repeat(jnp.arange(N, dtype=jnp.int64), DEG)
        W = jax.random.normal(k_w, (DOUT, DIN), dtype=jnp.float32) * std
        attn_l = jax.random.normal(k_al, (1, H, DOUT), dtype=jnp.float32) * std
        attn_r = jax.random.normal(k_ar, (1, H, DOUT), dtype=jnp.float32) * std
        W_res = jax.random.normal(k_wr, (DOUT, DIN), dtype=jnp.float32) * std
        return {'h': h, 'src': src, 'dst': dst, 'W': W, 'attn_l': attn_l, 'attn_r': attn_r, 'W_res': W_res}
    _L0_gnn_all = _L0_gnn_setup()
    _L0_gnn_in = {k: v for k, v in _L0_gnn_all.items() if k in ('W', 'attn_l', 'attn_r', 'W_res')}
    del _L0_gnn_all

    def _L0_ffn_setup():
        import jax, jax.numpy as jnp
        import numpy as np
        GT0 = [[0, 1, 0, 0, 1, 0], [0, 1, 0, 0, 0, 1], [0, 0, 1, 0, 1, 0], [0, 0, 1, 0, 0, 1], [0, 0, 0, 1, 1, 0], [0, 0, 0, 1, 0, 1]]
        NCLS = 6
        K = 1

        def _expert_pairs():
            pairs = []
            for i in range(NCLS):
                p = [(j - 1, k - 1) for j in range(1, 6) for k in range(1, 6) if j != k and GT0[i][j] == 1 and (GT0[i][k] == 1)]
                pairs.append(p)
            return pairs
        PAIRS = _expert_pairs()
        B, P, D, H = (64, 256, 768, 96)

        def _gelu(t):
            return jax.nn.gelu(t, approximate=False)
        key = jax.random.key(seed)
        ks = jax.random.split(key, 8)
        s = 0.02
        x = jax.random.normal(ks[0], (B, NCLS + P, D), dtype=jnp.float32)
        mids = jax.random.randint(ks[1], (B,), 0, 6)
        moe0_W1 = jax.random.normal(ks[2], (D, H), dtype=jnp.float32) * s
        moe0_b1 = jnp.zeros((H,), jnp.float32)
        moe0_W2 = jax.random.normal(ks[3], (H, D), dtype=jnp.float32) * s
        moe0_b2 = jnp.zeros((D,), jnp.float32)
        A1_W = jax.random.normal(ks[4], (5, D, H), dtype=jnp.float32) * s
        A1_b = jnp.zeros((5, H), jnp.float32)
        A2_W = jax.random.normal(ks[5], (5, H, D), dtype=jnp.float32) * s
        A2_b = jnp.zeros((5, D), jnp.float32)
        G_W = jax.random.normal(ks[6], (NCLS, D, 2), dtype=jnp.float32) * s
        return {'x': x, 'moe0_W1': moe0_W1, 'moe0_b1': moe0_b1, 'moe0_W2': moe0_W2, 'moe0_b2': moe0_b2, 'A1_W': A1_W, 'A1_b': A1_b, 'A2_W': A2_W, 'A2_b': A2_b, 'G_W': G_W, 'mids': mids}
    _L0_ffn_all = _L0_ffn_setup()
    _L0_ffn_in = {k: v for k, v in _L0_ffn_all.items() if k in ('moe0_W1', 'moe0_b1', 'moe0_W2', 'moe0_b2', 'A1_W', 'A1_b', 'A2_W', 'A2_b', 'G_W', 'mids')}
    del _L0_ffn_all
    return {'x': x, 'src': src, 'dst': dst, 'L0_gnn_W': _L0_gnn_in['W'], 'L0_gnn_attn_l': _L0_gnn_in['attn_l'], 'L0_gnn_attn_r': _L0_gnn_in['attn_r'], 'L0_gnn_W_res': _L0_gnn_in['W_res'], 'L0_ffn_moe0_W1': _L0_ffn_in['moe0_W1'], 'L0_ffn_moe0_b1': _L0_ffn_in['moe0_b1'], 'L0_ffn_moe0_W2': _L0_ffn_in['moe0_W2'], 'L0_ffn_moe0_b2': _L0_ffn_in['moe0_b2'], 'L0_ffn_A1_W': _L0_ffn_in['A1_W'], 'L0_ffn_A1_b': _L0_ffn_in['A1_b'], 'L0_ffn_A2_W': _L0_ffn_in['A2_W'], 'L0_ffn_A2_b': _L0_ffn_in['A2_b'], 'L0_ffn_G_W': _L0_ffn_in['G_W'], 'L0_ffn_mids': _L0_ffn_in['mids']}

def reference(x, src, dst, L0_gnn_W, L0_gnn_attn_l, L0_gnn_attn_r, L0_gnn_W_res, L0_ffn_moe0_W1, L0_ffn_moe0_b1, L0_ffn_moe0_W2, L0_ffn_moe0_b2, L0_ffn_A1_W, L0_ffn_A1_b, L0_ffn_A2_W, L0_ffn_A2_b, L0_ffn_G_W, L0_ffn_mids):
    import jax
    import jax.numpy as jnp

    def _L0_gnn_ref(h, src, dst, W, attn_l, attn_r, W_res):
        import jax, jax.numpy as jnp
        import numpy as np
        N = 625
        DEG = 16
        E = N * DEG
        H = 12
        DIN = 64
        DOUT = 64
        NEG_SLOPE = 0.2
        n = h.shape[0]
        hv = h.reshape(n, H, DIN)
        ft = jnp.einsum('nhd,od->nho', hv, W)
        a1 = jnp.sum(ft * attn_l, axis=-1)
        a2 = jnp.sum(ft * attn_r, axis=-1)
        e = jax.nn.leaky_relu(a1[src] + a2[dst], negative_slope=NEG_SLOPE)
        m = jax.ops.segment_max(e, dst, num_segments=n)
        m = jnp.where(jnp.isfinite(m), m, 0.0)
        w = jnp.exp(e - m[dst])
        denom = jax.ops.segment_sum(w, dst, num_segments=n)
        alpha = w / jnp.maximum(denom[dst], 1e-16)
        msg = alpha[:, :, None] * ft[src]
        agg = jax.ops.segment_sum(msg, dst, num_segments=n)
        res = jnp.einsum('nhd,od->nho', hv, W_res)
        out = jax.nn.relu((agg + res).reshape(n, H * DOUT))
        return out

    def _L0_ffn_ref(x, moe0_W1, moe0_b1, moe0_W2, moe0_b2, A1_W, A1_b, A2_W, A2_b, G_W, mids):
        import jax, jax.numpy as jnp
        import numpy as np
        GT0 = [[0, 1, 0, 0, 1, 0], [0, 1, 0, 0, 0, 1], [0, 0, 1, 0, 1, 0], [0, 0, 1, 0, 0, 1], [0, 0, 0, 1, 1, 0], [0, 0, 0, 1, 0, 1]]
        NCLS = 6
        K = 1

        def _expert_pairs():
            pairs = []
            for i in range(NCLS):
                p = [(j - 1, k - 1) for j in range(1, 6) for k in range(1, 6) if j != k and GT0[i][j] == 1 and (GT0[i][k] == 1)]
                pairs.append(p)
            return pairs
        PAIRS = _expert_pairs()
        B, P, D, H = (64, 256, 768, 96)

        def _gelu(t):
            return jax.nn.gelu(t, approximate=False)
        cls_tokens = x[:, :NCLS]
        patch_tokens = x[:, NCLS:]
        patch_out = _gelu(patch_tokens @ moe0_W1 + moe0_b1) @ moe0_W2 + moe0_b2
        cls_outs = []
        for i in range(NCLS):
            tok = cls_tokens[:, i]
            eouts = [_gelu(tok @ A1_W[a] + A1_b[a]) @ A2_W[c] + A2_b[c] for a, c in PAIRS[i]]
            out = jnp.stack(eouts, axis=-1)
            gate = jax.nn.softmax(tok @ G_W[i], axis=-1)
            thr = jnp.sort(gate, axis=-1)[..., -(K + 1)]
            mask = (gate > thr[..., None]).astype(gate.dtype)
            g = gate * mask
            g = g / jnp.clip(jnp.sum(g, axis=-1, keepdims=True), 1e-06)
            cls_outs.append(jnp.sum(out * g[:, None, :], axis=-1))
        cls_out = jnp.stack(cls_outs, axis=1)
        return jnp.concatenate([cls_out, patch_out], axis=1)
    x = x + _L0_gnn_ref(_layernorm(x, axis=-1), src, dst, L0_gnn_W, L0_gnn_attn_l, L0_gnn_attn_r, L0_gnn_W_res)
    x = x + _L0_ffn_ref(_layernorm(x, axis=-1)[None], L0_ffn_moe0_W1, L0_ffn_moe0_b1, L0_ffn_moe0_W2, L0_ffn_moe0_b2, L0_ffn_A1_W, L0_ffn_A1_b, L0_ffn_A2_W, L0_ffn_A2_b, L0_ffn_G_W, L0_ffn_mids)[0]
    return x

_drawn_inputs = setup_inputs


def setup_inputs(seed=0):
    import zlib

    import numpy as np

    out = dict(_drawn_inputs(seed))
    spreads = {'L0_ffn_moe0_b1': (0.0, 0.8),
     'L0_ffn_moe0_b2': (0.0, 0.1),
     'L0_ffn_A1_b': (0.0, 2.0),
     'L0_ffn_A2_b': (0.0, 2.0)}
    factors = {'L0_ffn_A1_W': 8.0, 'L0_ffn_A2_W': 8.0, 'L0_ffn_G_W': 22.46}
    for name, (base, spread) in spreads.items():
        noise = np.random.default_rng([zlib.crc32(name.encode()), seed]).standard_normal(out[name].shape)
        drawn = base * np.exp(spread * noise) if base else spread * noise
        out[name] = jnp.asarray(drawn.astype(out[name].dtype))
    for name, factor in factors.items():
        out[name] = (out[name] * factor).astype(out[name].dtype)
    return out
```

```python
import numpy as np
import concourse.bass as bass
from concourse import mybir
from contextlib import ExitStack

N_NODES = 50000
N_EDGES = 25000
D = 768
HEADS = 12
DH = D // HEADS
HID = 96
NCLS = 6
NEXP = 5
P = 128
NC = D // P
HC = P // DH

PAIR = 2
RING = 4
U = PAIR * RING
NT = -(-N_NODES // (P * U)) * U
NP = NT * P
EC = -(-N_EDGES // (P * RING)) * RING
EP = EC * P
PAD_NODE = NP - 1
NO_ROW = 1 << 20
BIG = 1e30
EPS = 1e-5
N_MEMSETS = 7
SLOPE = 0.2
REC = HEADS + 2

GT0 = [[0, 1, 0, 0, 1, 0], [0, 1, 0, 0, 0, 1], [0, 0, 1, 0, 1, 0],
       [0, 0, 1, 0, 0, 1], [0, 0, 0, 1, 1, 0], [0, 0, 0, 1, 0, 1]]
PAIRS = [[(j - 1, k - 1) for j in range(1, 6) for k in range(1, 6) if j != k and g[j] and g[k]] for g in GT0]


def turns(eng, n, drain):
    yield 0
    yield 1
    with eng.Fori(2, n) as b:
        yield b
    if drain:
        yield n


def settle(eng):
    eng.nop(nofuse=True)


def exists(t, n):
    return not isinstance(t, int) or 0 <= t < n


def at_least(eng, sem, value):
    if not isinstance(value, int) or value > 0:
        eng.wait_ge(sem, value)


def gnn_ffn_kernel(nc, x, edges, src_b, dst_a, dst_b, dst_next, dst_row, dst_first, dst_last,
                   eye, w_gnn, w_gnn_bd, w_res_bd, attn, w1, b1, w2, b2, a1w, a1b, a2w, a2b, gw, out):
    f32 = mybir.dt.float32
    i32 = mybir.dt.int32
    ALU = mybir.AluOpType
    ACT = mybir.ActivationFunctionType
    AX = mybir.AxisListType
    ds = bass.ds

    with ExitStack() as ctx:
        def sb(name, shape, dt=f32):
            return ctx.enter_context(nc.sbuf_tensor(name, shape, dt))

        def sem(name):
            return ctx.enter_context(nc.semaphore(name))

        rec_d = nc.dram_tensor("rec_scratch", [EP, REC], f32).ap()
        agg_d = nc.dram_tensor("agg_scratch", [EP, D], f32).ap()
        row_d = nc.dram_tensor("row_scratch", [NP, 1], i32).ap()
        cls_d = nc.dram_tensor("cls_scratch", [NCLS, D], f32).ap()

        x_ring = sb("x_ring", [P, U, D])
        g_ring = sb("g_ring", [P, U, D])
        y_ring = sb("y_ring", [P, U, D])
        n1 = sb("n1", [P, 2, D])
        n2 = sb("n2", [P, 2, D])
        t1 = sb("t1", [P, 2, D])
        t2 = sb("t2", [P, 2, D])
        o_buf = sb("o_buf", [P, RING, D])

        ident = sb("ident", [P, P])
        wg_bd = sb("wg_bd", [P, P])
        wr_bd = sb("wr_bd", [P, P])
        w_dup = sb("w_dup", [DH, P])
        attn_sb = sb("attn_sb", [DH, 2 * HEADS])
        v_sb = sb("v_sb", [P, NC * (2 * HEADS + 2)])
        ones = sb("ones", [P, P])
        sv = sb("sv", [P, 2 * HEADS])
        w1_sb = sb("w1_sb", [P, NC, HID])
        b1_sb = sb("b1_sb", [HID, 1])
        w2_sb = sb("w2_sb", [HID + 1, D])
        h_sb = sb("h_sb", [HID + 1, 2, P])
        half = sb("half", [P, EC])

        e_all = sb("e_all", [P, EC, 4], i32)
        e_slot = sb("e_slot", [P, RING, 4], i32)
        dsta = sb("dsta", [P, EC], i32)
        dstn = sb("dstn", [P, EC], i32)
        dstf = sb("dstf", [P, EC])
        tmp_f = sb("tmp_f", [P, EC])
        last_f = sb("last_f", [P, EC])
        bn_a = sb("bn_a", [P, 2, 2, 2, 6])
        mv_a = sb("mv_a", [P, 2, 4])
        scores = sb("scores", [P, 2 * HEADS, EC])
        mv = sb("mv", [P, 4, EC])
        rec = sb("rec", [P, EC, REC])
        same = sb("same", [P, EC])
        same_n = sb("same_n", [P, EC])
        in_first = sb("in_first", [P, EC])
        in_last = sb("in_last", [P, EC])
        pen = sb("pen", [P, EC])
        ends = sb("ends", [P, 2 * HEADS])
        carry_c = sb("carry_c", [P, 2 * HEADS])
        rowi = sb("rowi", [HEADS, 2, P], i32)
        rowf = sb("rowf", [HEADS, 2, P])
        link = sb("link", [HEADS, P + 1])
        whole = sb("whole", [HEADS, P])
        g_f = sb("g_f", [HEADS, P])
        g_b = sb("g_b", [HEADS, P])
        pens = sb("pens", [HEADS, 4, P])
        e_row = sb("e_row", [HEADS, 2, P])
        s_pad = sb("s_pad", [HEADS, P + 1])
        q_pad = sb("q_pad", [HEADS, P + 1])
        c_row = sb("c_row", [HEADS, 2, P])
        row_init = sb("row_init", [P, NT], i32)

        srcb = sb("srcb", [P, EC], i32)
        dstb = sb("dstb", [P, EC], i32)
        dstbf = sb("dstbf", [P, EC])
        rec_b = sb("rec_b", [P, RING, REC])
        row_b = sb("row_b", [P, RING, P], i32)
        same_m = sb("same_m", [P, 2, P])
        cont_m = sb("cont_m", [P, 2, P])

        nrow = sb("nrow", [P, U], i32)
        has = sb("has", [P, U])
        bn1 = sb("bn1", [P, 2, 2, 6])
        bn2 = sb("bn2", [P, 2, 2, 6])
        mv1 = sb("mv1", [P, U, 2])
        mv2 = sb("mv2", [P, U, 2])
        ve1 = sb("ve1", [P, U])
        ve2 = sb("ve2", [P, U])
        r1 = sb("r1", [P, U])
        r2 = sb("r2", [P, U])
        nm1 = sb("nm1", [P, U])
        nm2 = sb("nm2", [P, U])

        cls_t = sb("cls_t", [P, NC, NCLS])
        gw_sb = sb("gw_sb", [P, NC, NCLS * 2])
        a1_sb = sb("a1_sb", [P, NC, NEXP, HID])
        a1b_sb = sb("a1b_sb", [HID, NEXP])
        a2_sb = sb("a2_sb", [HID + 1, NEXP, D])
        hc = sb("hc", [HID + 1, NEXP, NCLS])
        hm = sb("hm", [HID + 1, 2, NEXP, NCLS])
        lg = sb("lg", [NCLS, NCLS, 2])
        gt = sb("gt", [NCLS, 16])
        flat_scores = scores[:, :, :].rearrange("p a b -> p (a b)")
        co = flat_scores[0:NCLS, 0:3 * D].rearrange("p (a c) -> p a c", a=3)
        cls_x = flat_scores[0:NCLS // PAIR, 3 * D:(3 + PAIR) * D].rearrange("p (a c) -> p a c", a=PAIR)

        ps = ctx.enter_context(nc.psum_tensor("ps", [P, 8, 512], f32))

        def pair(n):
            return ps[:, 2 * n:2 * n + 2, :].rearrange("p a b -> p (a b)")[:, 0:D]

        l_const = sem("l_const")
        l_edges = sem("l_edges")
        s_memset = sem("s_memset")
        s_attn = sem("s_attn")
        s_v = sem("s_v")
        s_sv = sem("s_sv")
        s_dve = sem("s_dve")
        s_rowinit = sem("s_rowinit")
        d_rowinit = sem("d_rowinit")
        s_eslot = sem("s_eslot")
        d_gs = [sem(f"d_gs{u}") for u in range(RING)]
        d_gd = [sem(f"d_gd{u}") for u in range(RING)]
        d_scat = [sem(f"d_scat{u}") for u in range(RING)]
        s_tps = sem("s_tps")
        s_tpd = sem("s_tpd")
        s_tes = sem("s_tes")
        s_ted = sem("s_ted")
        s_scs = sem("s_scs")
        s_scd = sem("s_scd")
        s_bna = sem("s_bna")
        s_aga = sem("s_aga")
        s_keep = sem("s_keep")
        s_va = sem("s_va")
        s_pow = sem("s_pow")
        s_ends = sem("s_ends")
        s_endt = sem("s_endt")
        s_crow = sem("s_crow")
        s_ccol = sem("s_ccol")
        s_z = sem("s_z")
        s_exp = sem("s_exp")
        s_rec = sem("s_rec")
        d_rec = sem("d_rec")
        s_bslot = sem("s_bslot")
        d_xg = [sem(f"d_xg{u}") for u in range(RING)]
        d_rb = [sem(f"d_rb{u}") for u in range(RING)]
        s_msg = sem("s_msg")
        s_masks = sem("s_masks")
        s_sum = sem("s_sum")
        s_run = sem("s_run")
        s_wag = sem("s_wag")
        s_aggo = sem("s_aggo")
        d_agg = [sem(f"d_agg{u}") for u in range(RING)]
        d_x = [sem(f"d_x{u}") for u in range(RING)]
        d_nr = [sem(f"d_nr{u}") for u in range(RING)]
        d_g = [sem(f"d_g{u}") for u in range(RING)]
        d_out = [sem(f"d_out{u}") for u in range(2)]
        s_bn1 = sem("s_bn1")
        s_ag1 = sem("s_ag1")
        s_ve1 = sem("s_ve1")
        s_r1 = sem("s_r1")
        s_nm1 = sem("s_nm1")
        s_n1 = sem("s_n1")
        s_tp1 = sem("s_tp1")
        s_te1 = sem("s_te1")
        s_res = sem("s_res")
        s_has = sem("s_has")
        s_add = sem("s_add")
        s_y = sem("s_y")
        s_bn2 = sem("s_bn2")
        s_ag2 = sem("s_ag2")
        s_ve2 = sem("s_ve2")
        s_r2 = sem("s_r2")
        s_nm2 = sem("s_nm2")
        s_n2 = sem("s_n2")
        s_tp2 = sem("s_tp2")
        s_te2 = sem("s_te2")
        s_up = sem("s_up")
        s_h = sem("s_h")
        s_down = sem("s_down")
        s_o = sem("s_o")
        l_cls = sem("l_cls")
        s_clsx = sem("s_clsx")
        d_clsx = sem("d_clsx")
        l_clsx = sem("l_clsx")
        s_clst = sem("s_clst")
        s_ch = sem("s_ch")
        s_cg = sem("s_cg")
        s_chg = sem("s_chg")
        s_chm = sem("s_chm")
        s_cmax = sem("s_cmax")
        s_cexp = sem("s_cexp")
        s_cs = sem("s_cs")
        s_cout = sem("s_cout")
        d_cls = sem("d_cls")

        x_v = x.rearrange("(q p k) c -> q p k c", p=P, k=PAIR)
        out_v = out.rearrange("(q p k) c -> q p k c", p=P, k=PAIR)
        row_v = row_d.rearrange("(q p k) c -> q p (k c)", p=P, k=PAIR)
        rec_bv = rec_d.rearrange("(c p) r -> c p r", p=P)
        agg_v = agg_d.rearrange("(c p) d -> c p d", p=P)
        NCONST = 14
        VW = 2 * HEADS + 2
        OFF = 2 * HEADS
        fwd = x_ring[:, :, :].rearrange("p a b -> p (a b)")[:, 0:HEADS * EC].rearrange("p (h e) -> p h e", h=HEADS)
        bwd = x_ring[:, :, :].rearrange("p a b -> p (a b)")[:, HEADS * EC:2 * HEADS * EC]\
            .rearrange("p (h e) -> p h e", h=HEADS)
        work = g_ring[:, :, :].rearrange("p a b -> p (a b)")[:, 0:HEADS * EC].rearrange("p (h e) -> p h e", h=HEADS)

        block = ctx.enter_context(nc.Block())

        @block.sync
        def _(sp):
            sp.dma_start(ident[:], eye).then_inc(l_const, 16)
            sp.dma_start(w_dup[:, 0:DH], w_gnn).then_inc(l_const, 16)
            sp.dma_start(w_dup[:, DH:P], w_gnn).then_inc(l_const, 16)
            sp.dma_start(attn_sb[:], attn).then_inc(l_const, 16)
            sp.dma_start(wg_bd[:], w_gnn_bd).then_inc(l_const, 16)
            sp.dma_start(wr_bd[:], w_res_bd).then_inc(l_const, 16)
            sp.dma_start(w1_sb[:], w1.rearrange("(c p) h -> p c h", p=P)).then_inc(l_const, 16)
            sp.dma_start(b1_sb[:], b1.rearrange("(p a) -> p a", a=1)).then_inc(l_const, 16)
            sp.dma_start(w2_sb[0:HID, :], w2).then_inc(l_const, 16)
            sp.dma_start(w2_sb[HID:HID + 1, :], b2.rearrange("(a c) -> a c", a=1)).then_inc(l_const, 16)
            sp.dma_start(rowi[:, 0, :], dst_first.to_broadcast([HEADS, P])).then_inc(l_const, 16)
            sp.dma_start(rowi[:, 1, :], dst_last.to_broadcast([HEADS, P])).then_inc(l_const, 16)
            sp.dma_start(srcb[:], src_b).then_inc(l_const, 16)
            sp.dma_start(dstb[:], dst_b).then_inc(l_const, 16)
            sp.dma_start(gw_sb[:], gw.rearrange("(c p) g -> p c g", p=P)).then_inc(l_cls, 16)
            sp.dma_start(a1_sb[:], a1w.rearrange("(c p) a h -> p c a h", p=P)).then_inc(l_cls, 16)
            sp.dma_start(a1b_sb[:], a1b).then_inc(l_cls, 16)
            sp.dma_start(a2_sb[0:HID, :, :], a2w).then_inc(l_cls, 16)
            sp.dma_start(a2_sb[HID:HID + 1, :, :], a2b.rearrange("(o a) d -> o a d", o=1)).then_inc(l_cls, 16)
            sp.wait_ge(s_rowinit, 1)
            sp.dma_start(row_d.rearrange("(p n) o -> p (n o)", p=P), row_init[:]).then_inc(d_rowinit, 16)
            sp.wait_ge(s_rec, 1)
            sp.dma_start(rec_d.rearrange("(p e) r -> p e r", p=P), rec[:]).then_inc(d_rec, 16)
            sp.wait_ge(d_rec, 16)
            for b in turns(sp, EC // RING, True):
                for u in range(RING):
                    c = b * RING + u
                    if exists(c, EC):
                        at_least(sp, s_masks, c - RING + 2)
                        sp.dma_start(rec_b[:, u, :], rec_bv[ds(c, 1)].rearrange("a p r -> p (a r)"))\
                            .then_inc(d_rb[u], 16)
                        sp.dma_start(row_b[:, u, :], dst_row[0:1, ds(c * P, P)].to_broadcast([P, P]))\
                            .then_inc(d_rb[u], 16)
                    co_ = c - 3
                    v = (u - 3) % RING
                    if exists(co_, EC):
                        sp.wait_ge(s_aggo, co_ + 1)
                        sp.dma_start(agg_v[ds(co_, 1)].rearrange("a p d -> p (a d)"), o_buf[:, v, :])\
                            .then_inc(d_agg[v], 16)
            for u in range(RING):
                sp.wait_ge(d_agg[u], 16 * (EC // RING))
            for u in range(RING):
                sp.wait_ge(d_scat[u], 16 * (EC // RING))
            for b in turns(sp, NT // U, True):
                for u in range(U):
                    t = b * U + u
                    if u % PAIR == 0 and exists(t, NT):
                        j = u // PAIR
                        at_least(sp, s_y, t - U + PAIR)
                        at_least(sp, s_has, t - U + PAIR)
                        at_least(sp, s_n1, t - U + PAIR)
                        sp.dma_start(x_ring[:, u:u + PAIR, :],
                                     x_v[ds(b * RING + j, 1)].rearrange("q p k c -> p (q k) c")).then_inc(d_x[j], 16)
                        at_least(sp, d_g[j], 32 * b)
                        sp.dma_start(nrow[:, u:u + PAIR],
                                     row_v[ds(b * RING + j, 1)].rearrange("q p k -> p (q k)")).then_inc(d_nr[j], 16)
                    to = t - 7
                    if (u - 7) % PAIR == 1 and exists(to, NT):
                        v = (u - 7) % U // PAIR
                        sp.wait_ge(s_o, to + 1)
                        s = v % 2
                        first = isinstance(b, int) and to == 1
                        lo = NCLS // PAIR if first else 0
                        pair_no = (to - 1) // PAIR if isinstance(b, int) else b * RING + (u - 8) // PAIR
                        sp.dma_start(out_v[ds(pair_no, 1), lo:P].rearrange("q p k c -> p (q k) c"),
                                     o_buf[lo:P, PAIR * s:PAIR * s + PAIR, :]).then_inc(d_out[s], 16)
            sp.wait_ge(s_clsx, PAIR)
            sp.dma_start(cls_d.rearrange("(p k) c -> p k c", k=PAIR), cls_x).then_inc(d_clsx, 16)
            sp.wait_ge(d_clsx, 16)
            sp.dma_start(co[:, 0, :], cls_d).then_inc(l_clsx, 16)
            for s in range(2):
                sp.wait_ge(d_out[s], 16 * (NT // U) * 2)
            sp.wait_ge(s_cout, 1)
            sp.dma_start(out[0:NCLS, :], co[:, 2, :]).then_inc(d_cls, 16)
            sp.wait_ge(d_cls, 16)

        @block.gpsimd
        def _(pool):
            pool.wait_ge(d_rowinit, 16)
            for b in turns(pool, EC // RING, False):
                for u in range(RING):
                    j = b * RING + u
                    pool.wait_ge(s_eslot, j + 1)
                    at_least(pool, s_tpd, j - RING + 1)
                    at_least(pool, s_aga, j - RING + 1)
                    settle(pool)
                    pool.indirect_dma_start(g_ring[:, u, :], None, x,
                                            bass.IndirectOffsetOnAxis(e_slot[:, u, 0:1], 0)).then_inc(d_gs[u], 16)
                    pool.indirect_dma_start(g_ring[:, RING + u, :], None, x,
                                            bass.IndirectOffsetOnAxis(e_slot[:, u, 1:2], 0)).then_inc(d_gd[u], 16)
                    pool.indirect_dma_start(row_d, bass.IndirectOffsetOnAxis(e_slot[:, u, 2:3], 0),
                                            e_slot[:, u, 3:4], None, bounds_check=NP - 1, oob_is_err=False)\
                        .then_inc(d_scat[u], 16)
            for n in range(2):
                pool.wait_ge(s_va, n + 1)
                pool.tensor_tensor(mv[:, 2 * n + 1, :], mv[:, 2 * n + 1, :], half[:], ALU.pow).then_inc(s_pow, 1)
            pool.wait_ge(s_rec, 1)
            for b in turns(pool, EC // RING, False):
                for u in range(RING):
                    c = b * RING + u
                    pool.wait_ge(s_bslot, c + 1)
                    at_least(pool, s_msg, c - RING + 1)
                    settle(pool)
                    pool.indirect_dma_start(g_ring[:, u, :], None, x,
                                            bass.IndirectOffsetOnAxis(e_slot[:, u, 0:1], 0)).then_inc(d_xg[u], 16)
            for u in range(RING):
                pool.wait_ge(d_agg[u], 16 * (EC // RING))
            pool.wait_ge(s_msg, EC)
            for b in turns(pool, NT // U, True):
                for u in range(U):
                    t = b * U + u
                    if u % PAIR == 0 and exists(t, NT):
                        j = u // PAIR
                        pool.wait_ge(d_nr[j], 16 * b + 16)
                        at_least(pool, s_add, t - U + PAIR)
                        for k in range(PAIR):
                            settle(pool)
                            pool.indirect_dma_start(g_ring[:, u + k, :], None, agg_d,
                                                    bass.IndirectOffsetOnAxis(nrow[:, u + k:u + k + 1], 0),
                                                    bounds_check=EP - 1, oob_is_err=False).then_inc(d_g[j], 16)
                    if exists(t, NT):
                        pool.wait_ge(s_ve1, t + 1)
                        settle(pool)
                        pool.tensor_tensor(r1[:, u:u + 1], ve1[:, u:u + 1], half[:, 0:1], ALU.pow).then_inc(s_r1, 1)
                    tn = t - 1
                    if exists(tn, NT):
                        v = (u - 1) % U
                        pool.wait_ge(s_nm1, tn + 1)
                        at_least(pool, s_tp1, tn - 1)
                        settle(pool)
                        pool.tensor_scalar(n1[:, v % 2, :], x_ring[:, v, :], r1[:, v:v + 1], nm1[:, v:v + 1],
                                           ALU.mult, ALU.add).then_inc(s_n1, 1)
                    ty = t - 4
                    if exists(ty, NT):
                        v = (u - 4) % U
                        pool.wait_ge(s_nm2, ty + 1)
                        at_least(pool, s_tp2, ty - 1)
                        settle(pool)
                        pool.tensor_scalar(n2[:, v % 2, :], y_ring[:, v, :], r2[:, v:v + 1], nm2[:, v:v + 1],
                                           ALU.mult, ALU.add).then_inc(s_n2, 1)
                    tp = t - 3
                    if exists(tp, NT):
                        v = (u - 3) % U
                        pool.wait_ge(s_ve2, tp + 1)
                        settle(pool)
                        pool.tensor_tensor(r2[:, v:v + 1], ve2[:, v:v + 1], half[:, 0:1], ALU.pow).then_inc(s_r2, 1)

        @block.scalar
        def _(act):
            act.dma_start(e_all[:], edges).then_inc(l_edges, 16)
            act.dma_start(dsta[:], dst_a).then_inc(l_edges, 16)
            act.dma_start(dstn[:], dst_next).then_inc(l_edges, 16)
            for b in turns(act, EC // RING, True):
                for u in range(RING):
                    j = b * RING + u
                    if exists(j, EC):
                        act.wait_ge(s_tps, j + 1)
                        at_least(act, s_scs, j)
                        nc.scalar.activation(t1[:, 0, :], pair(0), ACT.Copy).then_inc(s_tes, 1)
                        act.wait_ge(s_tpd, j + 1)
                        at_least(act, s_scd, j)
                        nc.scalar.activation(t1[:, 1, :], pair(1), ACT.Copy).then_inc(s_ted, 1)
            act.wait_ge(s_z, 1)
            nc.scalar.activation(scores[:, 0:HEADS, :], fwd, ACT.Exp).then_inc(s_exp, 1)
            for b in turns(act, EC // RING, False):
                for u in range(RING):
                    c = b * RING + u
                    act.wait_ge(s_wag, c + 1)
                    at_least(act, d_agg[u], 16 * b)
                    nc.scalar.activation(o_buf[:, u, :], pair(2 + u % 2), ACT.Copy).then_inc(s_aggo, 1)
            for b in turns(act, NT // U, True):
                for u in range(U):
                    t = b * U + u
                    ta = t - 2
                    if exists(ta, NT):
                        act.wait_ge(s_tp1, ta + 1)
                        at_least(act, s_res, ta - 1)
                        nc.scalar.activation(t1[:, u % 2, :], pair(0), ACT.Copy).then_inc(s_te1, 1)
                    tb = t - 5
                    if exists(tb, NT):
                        act.wait_ge(s_tp2, tb + 1)
                        at_least(act, s_up, tb - 1)
                        nc.scalar.activation(t2[:, (u - 5) % 2, :], pair(0), ACT.Copy).then_inc(s_te2, 1)
                        if isinstance(b, int) and tb < PAIR:
                            act.wait_ge(s_te2, tb + 1)
                            nc.scalar.activation(cls_t[:, :, tb:NCLS:PAIR],
                                                 t2[:, (u - 5) % 2, :].rearrange("p (c n) -> p c n", c=NC)[:, :, 0:NCLS // PAIR],
                                                 ACT.Copy).then_inc(s_clst, 1)
                    th = t - 6
                    if exists(th, NT):
                        v = (u - 6) % 2
                        act.wait_ge(s_up, th + 1)
                        at_least(act, s_down, th - 1)
                        nc.scalar.activation(h_sb[0:HID, v, :], ps[0:HID, 6 + v, 0:P], ACT.Gelu, bias=b1_sb[:])\
                            .then_inc(s_h, 1)
            act.wait_ge(l_cls, 16 * 5)
            act.wait_ge(s_ch, 1)
            for a in range(NEXP):
                nc.scalar.activation(hc[0:HID, a, :], ps[0:HID, 0, a * NCLS:(a + 1) * NCLS], ACT.Gelu,
                                     bias=a1b_sb[:, a:a + 1]).then_inc(s_chg, 1)
            act.wait_ge(s_cmax, 1)
            nc.scalar.activation(gt[:, 4:6], gt[:, 0:2], ACT.Exp).then_inc(s_cexp, 1)

        @block.tensor
        def _(pe):
            pe.wait_ge(l_const, 16 * NCONST)
            pe.wait_ge(s_memset, N_MEMSETS)
            nc.tensor.matmul(ps[:, 0, 0:2 * HEADS], w_dup[:], attn_sb[:], start=True, stop=True).then_inc(s_attn, 1)
            pe.wait_ge(s_v, 4)
            for c in range(NC):
                last = nc.tensor.matmul(ps[:, 1, 0:2 * HEADS], ones[:], v_sb[:, OFF * c:OFF * c + OFF],
                                        start=(c == 0), stop=(c == NC - 1))
            last.then_inc(s_sv, 1)
            pe.wait_ge(s_v, 5)

            def transposes(dst, src, done):
                for c in range(NC):
                    last = nc.tensor.transpose(dst[:, c * P:(c + 1) * P], src[:, c * P:(c + 1) * P], ident[:])
                last.then_inc(done, 1)

            def score(dst, src, off, done):
                for c in range(NC):
                    last = nc.tensor.matmul(dst, src[:, c * P:(c + 1) * P],
                                            v_sb[:, OFF * c + off:OFF * c + off + HEADS],
                                            start=(c == 0), stop=(c == NC - 1))
                last.then_inc(done, 1)

            for b in turns(pe, EC // RING, True):
                for u in range(RING):
                    j = b * RING + u
                    if exists(j, EC):
                        pe.wait_ge(d_gs[u], 16 * b + 16)
                        at_least(pe, s_tes, j)
                        transposes(pair(0), g_ring[:, u, :], s_tps)
                    jd = j - 1
                    if exists(jd, EC):
                        pe.wait_ge(s_ted, jd + 1)
                        score(ps[:, 4 + (u - 1) % 2, HEADS:2 * HEADS], t1[:, 1, :], HEADS, s_scd)
                    if exists(j, EC):
                        pe.wait_ge(d_gd[u], 16 * b + 16)
                        at_least(pe, s_ted, j)
                        transposes(pair(1), g_ring[:, RING + u, :], s_tpd)
                        pe.wait_ge(s_tes, j + 1)
                        at_least(pe, s_keep, j - 1)
                        score(ps[:, 4 + u % 2, 0:HEADS], t1[:, 0, :], 0, s_scs)
            for n in range(2):
                pe.wait_ge(s_ends, n + 1)
                for i in range(2):
                    last = nc.tensor.transpose(ps[0:HEADS, 6, i * P:(i + 1) * P],
                                               ends[:, i * HEADS:(i + 1) * HEADS], ident[:])
                last.then_inc(s_endt, 1)
                pe.wait_ge(s_crow, n + 1)
                for i in range(2):
                    last = nc.tensor.transpose(ps[:, 7, i * HEADS:(i + 1) * HEADS], c_row[:, i, :],
                                               ident[0:HEADS, 0:HEADS])
                last.then_inc(s_ccol, 1)
            for b in turns(pe, EC // RING, True):
                for u in range(RING):
                    c = b * RING + u
                    if exists(c, EC):
                        pe.wait_ge(s_msg, c + 1)
                        pe.wait_ge(s_masks, c + 1)
                        at_least(pe, s_run, c - 1)
                        for i in range(NC):
                            last = nc.tensor.matmul(pair(u % 2)[:, i * P:(i + 1) * P],
                                                    y_ring[:, u % 2, i * P:(i + 1) * P], same_m[:, u % 2, :],
                                                    start=True, stop=True)
                        last.then_inc(s_sum, 1)
                    cw = c - 1
                    if exists(cw, EC):
                        v = (u - 1) % 2
                        pe.wait_ge(s_run, cw + 1)
                        at_least(pe, s_aggo, cw - 1)
                        for i in range(NC):
                            last = nc.tensor.matmul(pair(2 + v)[:, i * P:(i + 1) * P],
                                                    y_ring[:, 2 + v, i * P:(i + 1) * P], wg_bd[:],
                                                    start=True, stop=True)
                        last.then_inc(s_wag, 1)
            pe.wait_ge(s_aggo, EC)
            for b in turns(pe, NT // U, True):
                for u in range(U):
                    t = b * U + u
                    ta = t - 2
                    if exists(ta, NT):
                        pe.wait_ge(s_n1, ta + 1)
                        at_least(pe, s_te2, ta - 3)
                        if isinstance(b, int) and b == 0:
                            at_least(pe, s_te1, ta)
                        transposes(pair(0), n1[:, u % 2, :], s_tp1)
                    tr = t - 3
                    if exists(tr, NT):
                        pe.wait_ge(s_te1, tr + 1)
                        at_least(pe, s_add, tr)
                        for i in range(NC):
                            last = nc.tensor.matmul(pair(1)[:, i * P:(i + 1) * P],
                                                    t1[:, (u - 3) % 2, i * P:(i + 1) * P], wr_bd[:],
                                                    start=True, stop=True)
                        last.then_inc(s_res, 1)
                    tb = t - 5
                    if exists(tb, NT):
                        pe.wait_ge(s_n2, tb + 1)
                        if isinstance(b, int) and t - 2 >= NT:
                            pe.wait_ge(s_te1, NT)
                            at_least(pe, s_te2, tb)
                        else:
                            pe.wait_ge(s_te1, ta + 1)
                        transposes(pair(0), n2[:, (u - 5) % 2, :], s_tp2)
                    tu = t - 6
                    if exists(tu, NT):
                        v = (u - 6) % 2
                        pe.wait_ge(s_te2, tu + 1)
                        at_least(pe, s_h, tu - 1)
                        for i in range(NC):
                            last = nc.tensor.matmul(ps[0:HID, 6 + v, 0:P], w1_sb[:, i, :],
                                                    t2[:, v, i * P:(i + 1) * P],
                                                    start=(i == 0), stop=(i == NC - 1))
                        last.then_inc(s_up, 1)
                    td = t - 7
                    if exists(td, NT):
                        v = (u - 7) % 2
                        pe.wait_ge(s_h, td + 1)
                        at_least(pe, s_o, td)
                        nc.tensor.matmul(pair(2)[:, 0:512], h_sb[:, v, :], w2_sb[:, 0:512], start=True, stop=True)
                        nc.tensor.matmul(pair(2)[:, 512:D], h_sb[:, v, :], w2_sb[:, 512:D], start=True, stop=True)\
                            .then_inc(s_down, 1)
            pe.wait_ge(s_te2, NT)
            pe.wait_ge(l_cls, 16 * 5)
            pe.wait_ge(s_clst, PAIR)
            for a in range(NEXP):
                for i in range(NC):
                    last = nc.tensor.matmul(ps[0:HID, 0, a * NCLS:(a + 1) * NCLS], a1_sb[:, i, a, :], cls_t[:, i, :],
                                            start=(i == 0), stop=(i == NC - 1))
            last.then_inc(s_ch, 1)
            for i in range(NC):
                last = nc.tensor.matmul(ps[0:NCLS, 1, 0:2 * NCLS], cls_t[:, i, :], gw_sb[:, i, :],
                                        start=(i == 0), stop=(i == NC - 1))
            last.then_inc(s_cg, 1)
            pe.wait_ge(s_chm, 1)
            pe.wait_ge(s_o, NT)
            for s in range(2):
                for lo, hi in ((0, 512), (512, D)):
                    for a in range(NEXP):
                        last = nc.tensor.matmul(pair(1 + s)[0:NCLS, lo:hi], hm[:, s, a, :], a2_sb[:, a, lo:hi],
                                                start=(a == 0), stop=(a == NEXP - 1))
            last.then_inc(s_cs, 1)

        @block.vector
        def _(dve):
            done = [0]

            def link_up(ins):
                done[0] += 1
                ins.then_inc(s_dve, 1)
                dve.wait_ge(s_dve, done[0])

            V = nc.vector
            V.memset(ones[:], 1.0).then_inc(s_memset, 1)
            V.memset(v_sb[:], 0.0).then_inc(s_memset, 1)
            V.memset(half[:], -0.5).then_inc(s_memset, 1)
            V.memset(h_sb[HID:HID + 1, :, :], 1.0).then_inc(s_memset, 1)
            V.memset(rec[:, :, HEADS:REC], 0.0).then_inc(s_memset, 1)
            V.memset(row_init[:], NO_ROW).then_inc(s_rowinit, 1)
            V.memset(hc[HID:HID + 1, :, :], 1.0).then_inc(s_memset, 1)
            V.memset(hm[:], 0.0).then_inc(s_memset, 1)
            dve.wait_ge(s_memset, N_MEMSETS)
            dve.wait_ge(l_const, 16 * NCONST)
            dve.wait_ge(s_attn, 1)
            v26 = v_sb[:, :].rearrange("p (c w) -> p c w", w=VW)
            for par in range(HC):
                rows = slice(par * DH, (par + 1) * DH)
                for side in range(2):
                    V.tensor_copy(v26[rows, :, side * HEADS + par],
                                  ps[rows, 0, side * HEADS + par:(side + 1) * HEADS:HC]).then_inc(s_v, 1)
            dve.wait_ge(s_sv, 1)
            V.tensor_copy(sv[:], ps[:, 1, 0:2 * HEADS]).then_inc(s_v, 1)
            dve.wait_ge(l_edges, 16 * 3)
            link_up(V.tensor_copy(dstf[:], dsta[:]))
            link_up(V.tensor_copy(tmp_f[:], dstn[:]))
            link_up(V.tensor_tensor(last_f[:], dstf[:], tmp_f[:], ALU.is_equal))
            link_up(V.scalar_tensor_tensor(tmp_f[:], last_f[:], float(NO_ROW), dstf[:], ALU.mult, ALU.add))
            link_up(V.tensor_copy(e_all[:, :, 2], tmp_f[:]))
            link_up(V.tensor_copy(dstbf[:], dstb[:]))
            for b in turns(dve, EC // RING, True):
                for u in range(RING):
                    j = b * RING + u
                    if exists(j, EC):
                        at_least(dve, d_gs[u], 16 * b)
                        at_least(dve, d_gd[u], 16 * b)
                        at_least(dve, d_scat[u], 16 * b)
                        V.tensor_copy(e_slot[:, u, :], e_all[:, ds(j, 1), :].rearrange("p a b -> p (a b)"))\
                            .then_inc(s_eslot, 1)
                    jb = j - 2
                    if exists(jb, EC):
                        v = (u - 2) % RING
                        w = v % 2
                        n = (b * 16 + 16) if u >= 2 else (b * 16)
                        dve.wait_ge(d_gs[v], n)
                        dve.wait_ge(d_gd[v], n)
                        for side in range(2):
                            for h in range(2):
                                V.bn_stats(bn_a[:, w, side, h, :],
                                           g_ring[:, side * RING + v, h * (D // 2):(h + 1) * (D // 2)]).then_inc(s_bna, 1)
                        dve.wait_ge(s_bna, jb * 4 + 4)
                        for side in range(2):
                            settle(dve)
                            last = V.bn_aggr(mv_a[:, w, 2 * side:2 * side + 2],
                                             bn_a[:, w, side, :, :].rearrange("p a b -> p (a b)"))
                        last.then_inc(s_aga, 1)
                        dve.wait_ge(s_aga, jb + 1)
                        V.tensor_copy(mv[:, :, ds(jb, 1)].rearrange("p a b -> p (a b)"), mv_a[:, w, :])
                    jk = j - 3
                    if exists(jk, EC):
                        w = (u - 3) % 2
                        dve.wait_ge(s_scs, jk + 1)
                        dve.wait_ge(s_scd, jk + 1)
                        V.tensor_copy(scores[:, :, ds(jk, 1)].rearrange("p a b -> p (a b)"), ps[:, 4 + w, 0:2 * HEADS])\
                            .then_inc(s_keep, 1)
            dve.wait_ge(s_keep, EC)
            for n in range(2):
                V.tensor_scalar(mv[:, 2 * n + 1, :], mv[:, 2 * n + 1, :], EPS, None, ALU.add).then_inc(s_va, 1)
            link_up(V.memset(same[:, 0:1], 0.0))
            link_up(V.tensor_tensor(same[:, 1:EC], dstf[:, 1:EC], dstf[:, 0:EC - 1], ALU.is_equal))
            link_up(V.memset(same_n[:, EC - 1:EC], 0.0))
            link_up(V.tensor_copy(same_n[:, 0:EC - 1], same[:, 1:EC]))
            link_up(V.tensor_scalar(in_first[:], dstf[:], dstf[:, 0:1], None, ALU.is_equal))
            link_up(V.tensor_scalar(in_last[:], dstf[:], dstf[:, EC - 1:EC], None, ALU.is_equal))
            link_up(V.tensor_copy(rowf[:], rowi[:]))
            link_up(V.memset(link[:], 0.0))
            link_up(V.tensor_tensor(link[:, 1:P], rowf[:, 0, 1:P], rowf[:, 1, 0:P - 1], ALU.is_equal))
            link_up(V.tensor_tensor(whole[:], rowf[:, 0, :], rowf[:, 1, :], ALU.is_equal))
            link_up(V.tensor_tensor(g_f[:], whole[:], link[:, 0:P], ALU.mult))
            link_up(V.tensor_tensor(g_b[:], whole[:], link[:, 1:P + 1], ALU.mult))
            for n, m in enumerate((g_f[:], g_b[:], link[:, 0:P], link[:, 1:P + 1])):
                link_up(V.tensor_scalar(pens[:, n, :], m, 1.0, BIG, ALU.subtract, ALU.mult))
            link_up(V.memset(s_pad[:], 0.0))
            link_up(V.memset(q_pad[:], 0.0))
            dve.wait_ge(s_pow, 2)
            dve.wait_ge(s_v, 5)

            def per_edge(row):
                return row[:, None, :].to_broadcast([P, HEADS, EC])

            def per_head(col):
                return col[:, :, None].to_broadcast([P, HEADS, EC])

            for n in range(2):
                part = scores[:, n * HEADS:(n + 1) * HEADS, :]
                link_up(V.tensor_tensor(fwd, per_edge(mv[:, 2 * n, :]), per_head(sv[:, n * HEADS:(n + 1) * HEADS]),
                                        ALU.mult))
                link_up(V.tensor_tensor(part, part, fwd, ALU.subtract))
                link_up(V.tensor_tensor(part, part, per_edge(mv[:, 2 * n + 1, :]), ALU.mult))
            e_v = scores[:, 0:HEADS, :]
            a2_v = scores[:, HEADS:2 * HEADS, :]
            link_up(V.tensor_tensor(fwd, e_v, a2_v, ALU.add))
            link_up(V.scalar_tensor_tensor(e_v.rearrange("p h e -> p (h e)"), fwd.rearrange("p h e -> p (h e)"), SLOPE,
                                           fwd.rearrange("p h e -> p (h e)"), ALU.mult, ALU.max))

            def scan(out_, d0, d1, init, op0, op1):
                for h in range(HEADS):
                    last = V.tensor_tensor_scan(out_(h), d0, d1(h), init, op0, op1)
                link_up(last)

            def carries(n, g0, g1, ops):
                link_up(V.tensor_copy(ends[:, 0:HEADS], fwd[:, :, EC - 1]))
                V.tensor_copy(ends[:, HEADS:2 * HEADS], bwd[:, :, 0]).then_inc(s_ends, 1)
                dve.wait_ge(s_endt, n + 1)
                link_up(V.tensor_copy(e_row[:].rearrange("h a b -> h (a b)"), ps[0:HEADS, 6, 0:2 * P]))
                link_up(V.tensor_tensor_scan(s_pad[:, 1:P + 1], g0, e_row[:, 0, :], 0.0, *ops))
                link_up(V.tensor_tensor_scan(q_pad[:, 0:P][:, ::-1], g1[:, ::-1],
                                             e_row[:, 1, ::-1], 0.0, *ops))

            link_up(V.tensor_scalar(pen[:], same[:], 1.0, BIG, ALU.subtract, ALU.mult))
            scan(lambda h: fwd[:, h, :], pen[:], lambda h: e_v[:, h, :], -BIG, ALU.add, ALU.max)
            link_up(V.tensor_scalar(pen[:], same_n[:], 1.0, BIG, ALU.subtract, ALU.mult))
            scan(lambda h: bwd[:, h, ::-1], pen[:, ::-1], lambda h: fwd[:, h, ::-1], -BIG, ALU.add, ALU.max)
            carries(0, pens[:, 0, :], pens[:, 1, :], (ALU.add, ALU.max))
            link_up(V.tensor_tensor(c_row[:, 0, :], s_pad[:, 0:P], pens[:, 2, :], ALU.add))
            V.tensor_tensor(c_row[:, 1, :], q_pad[:, 1:P + 1], pens[:, 3, :], ALU.add).then_inc(s_crow, 1)
            dve.wait_ge(s_ccol, 1)
            link_up(V.tensor_copy(carry_c[:], ps[:, 7, 0:2 * HEADS]))
            for side, inside in enumerate((in_first, in_last)):
                link_up(V.tensor_scalar(pen[:], inside[:], 1.0, BIG, ALU.subtract, ALU.mult))
                link_up(V.tensor_tensor(work, per_head(carry_c[:, side * HEADS:(side + 1) * HEADS]), per_edge(pen[:]),
                                        ALU.add))
                link_up(V.tensor_tensor(bwd, bwd, work, ALU.max))
            V.tensor_tensor(fwd, e_v, bwd, ALU.subtract).then_inc(s_z, 1)
            dve.wait_ge(s_exp, 1)
            scan(lambda h: fwd[:, h, :], same[:], lambda h: e_v[:, h, :], 0.0, ALU.mult, ALU.add)
            scan(lambda h: bwd[:, h, ::-1], same_n[:, ::-1], lambda h: fwd[:, h, ::-1], 0.0, ALU.mult, ALU.max)
            carries(1, g_f[:], g_b[:], (ALU.mult, ALU.add))
            link_up(V.tensor_tensor(c_row[:, 0, :], s_pad[:, 0:P], link[:, 0:P], ALU.mult))
            V.tensor_tensor(c_row[:, 1, :], q_pad[:, 1:P + 1], link[:, 1:P + 1], ALU.mult).then_inc(s_crow, 1)
            dve.wait_ge(s_ccol, 2)
            link_up(V.tensor_copy(carry_c[:], ps[:, 7, 0:2 * HEADS]))
            for side, inside in enumerate((in_first, in_last)):
                link_up(V.tensor_tensor(work, per_head(carry_c[:, side * HEADS:(side + 1) * HEADS]),
                                        per_edge(inside[:]), ALU.mult))
                link_up(V.tensor_tensor(bwd, bwd, work, ALU.add))
            link_up(V.tensor_scalar(bwd, bwd, 1e-16, None, ALU.max))
            link_up(V.reciprocal(fwd, bwd))
            link_up(V.tensor_tensor(fwd, fwd, e_v, ALU.mult))
            link_up(V.tensor_tensor(rec[:, :, 0:HEADS].rearrange("p e h -> p h e"), fwd, per_edge(mv[:, 1, :]), ALU.mult))
            V.tensor_copy(rec[:, :, HEADS], mv[:, 0, :]).then_inc(s_rec, 1)
            for u in range(RING):
                dve.wait_ge(d_scat[u], 16 * (EC // RING))
            for b in turns(dve, EC // RING, True):
                for u in range(RING):
                    c = b * RING + u
                    if exists(c, EC):
                        at_least(dve, d_xg[u], 16 * b)
                        V.tensor_copy(e_slot[:, u, 0:1], srcb[:, ds(c, 1)]).then_inc(s_bslot, 1)
                    cm = c - 2
                    if exists(cm, EC):
                        v = (u - 2) % RING
                        w = v % 2
                        n = b + 1 if u >= 2 else b
                        dve.wait_ge(d_xg[v], n * 16)
                        dve.wait_ge(d_rb[v], n * 32)
                        at_least(dve, s_sum, cm - 1)
                        V.scalar_tensor_tensor(
                            y_ring[:, w, :].rearrange("p (h d) -> p h d", h=HEADS),
                            g_ring[:, v, :].rearrange("p (h d) -> p h d", h=HEADS), rec_b[:, v, HEADS:HEADS + 1],
                            rec_b[:, v, 0:HEADS][:, :, None].to_broadcast([P, HEADS, DH]), ALU.subtract, ALU.mult)\
                            .then_inc(s_msg, 1)
                        at_least(dve, s_run, cm - 1)
                        V.tensor_scalar(same_m[:, w, :], row_b[:, v, :], dstbf[:, ds(cm, 1)], None, ALU.is_equal)
                        if isinstance(cm, int) and cm == 0:
                            V.memset(cont_m[:, w, :], 0.0).then_inc(s_masks, 1)
                        else:
                            V.tensor_scalar(cont_m[:, w, :], row_b[:, v, :], row_b[:, (v - 1) % RING, P - 1:P], None,
                                            ALU.is_equal).then_inc(s_masks, 1)
                    cr = c - 3
                    if exists(cr, EC):
                        w = (u - 3) % 2
                        dve.wait_ge(s_sum, cr + 1)
                        dve.wait_ge(s_masks, cr + 1)
                        at_least(dve, s_wag, cr - 1)
                        at_least(dve, s_run, cr)
                        if isinstance(cr, int) and cr == 0:
                            last = V.tensor_copy(y_ring[:, 2 + w, :], pair(w))
                        else:
                            for i in range(NC):
                                last = V.scalar_tensor_tensor(
                                    y_ring[:, 2 + w, i * P:(i + 1) * P], cont_m[:, w, :],
                                    y_ring[:, 3 - w, (i + 1) * P - 1:(i + 1) * P],
                                    pair(w)[:, i * P:(i + 1) * P], ALU.mult, ALU.add)
                        last.then_inc(s_run, 1)
            dve.wait_ge(s_wag, EC)
            for u in range(RING):
                dve.wait_ge(d_agg[u], 16 * (EC // RING))
            for b in turns(dve, NT // U, True):
                for u in range(U):
                    t = b * U + u
                    if exists(t - 1, NT):
                        v = (u - 1) % U
                        dve.wait_ge(s_r1, t)
                        V.scalar_tensor_tensor(nm1[:, v:v + 1], mv1[:, v, 0:1], -1.0, r1[:, v:v + 1],
                                               ALU.mult, ALU.mult).then_inc(s_nm1, 1)
                    if exists(t - 4, NT):
                        v = (u - 4) % U
                        dve.wait_ge(s_r2, t - 3)
                        V.scalar_tensor_tensor(nm2[:, v:v + 1], mv2[:, v, 0:1], -1.0, r2[:, v:v + 1],
                                               ALU.mult, ALU.mult).then_inc(s_nm2, 1)
                    if exists(t, NT):
                        j = u // PAIR
                        if u % PAIR == 0:
                            dve.wait_ge(d_x[j], 16 * b + 16)
                            dve.wait_ge(d_nr[j], 16 * b + 16)
                            at_least(dve, s_add, t - U + PAIR)
                            V.tensor_scalar(has[:, u:u + PAIR], nrow[:, u:u + PAIR], float(EP), None, ALU.is_lt)\
                                .then_inc(s_has, PAIR)
                        for h in range(2):
                            V.bn_stats(bn1[:, u % 2, h, :], x_ring[:, u, h * (D // 2):(h + 1) * (D // 2)])\
                                .then_inc(s_bn1, 1)
                        dve.wait_ge(s_bn1, 2 * t + 2)
                        at_least(dve, s_nm1, t - U + 1)
                        settle(dve)
                        V.bn_aggr(mv1[:, u, :], bn1[:, u % 2, :, :].rearrange("p a b -> p (a b)")).then_inc(s_ag1, 1)
                        dve.wait_ge(s_ag1, t + 1)
                        V.tensor_scalar(ve1[:, u:u + 1], mv1[:, u, 1:2], EPS, None, ALU.add).then_inc(s_ve1, 1)
                    tr = t - 3
                    if exists(tr, NT):
                        v = (u - 3) % U
                        if v % PAIR == 0:
                            n = b + 1 if u >= 3 else b
                            dve.wait_ge(d_g[v // PAIR], 32 * n)
                            dve.wait_ge(s_has, tr + PAIR)
                        dve.wait_ge(s_res, tr + 1)
                        at_least(dve, s_o, tr - U + 1)
                        V.scalar_tensor_tensor(y_ring[:, v, :], g_ring[:, v, :], has[:, v:v + 1], pair(1),
                                               ALU.mult, ALU.add).then_inc(s_add, 1)
                        dve.wait_ge(s_add, tr + 1)
                        V.scalar_tensor_tensor(y_ring[:, v, :], y_ring[:, v, :], 0.0, x_ring[:, v, :],
                                               ALU.max, ALU.add).then_inc(s_y, 1)
                        dve.wait_ge(s_y, tr + 1)
                        for h in range(2):
                            V.bn_stats(bn2[:, v % 2, h, :], y_ring[:, v, h * (D // 2):(h + 1) * (D // 2)])\
                                .then_inc(s_bn2, 1)
                        dve.wait_ge(s_bn2, 2 * tr + 2)
                        settle(dve)
                        V.bn_aggr(mv2[:, v, :], bn2[:, v % 2, :, :].rearrange("p a b -> p (a b)")).then_inc(s_ag2, 1)
                        dve.wait_ge(s_ag2, tr + 1)
                        V.tensor_scalar(ve2[:, v:v + 1], mv2[:, v, 1:2], EPS, None, ALU.add).then_inc(s_ve2, 1)
                        if isinstance(tr, int) and tr < PAIR:
                            V.tensor_copy(cls_x[:, tr, :], y_ring[0:NCLS // PAIR, v, :]).then_inc(s_clsx, 1)
                    td = t - 7
                    if exists(td, NT):
                        v = (u - 7) % U
                        s = v % (2 * PAIR)
                        dve.wait_ge(s_down, td + 1)
                        if s % PAIR == 0:
                            if not isinstance(td, int):
                                k = v // PAIR
                                turn = b if u == 7 else b - 1
                                dve.wait_ge(d_out[s // PAIR], 16 * (2 * turn + k // 2))
                            elif td >= 2 * PAIR:
                                dve.wait_ge(d_out[s // PAIR], 16 * (td // PAIR // 2))
                        V.tensor_tensor(o_buf[:, s, :], y_ring[:, v, :], pair(2), ALU.add).then_inc(s_o, 1)
            dve.wait_ge(s_chg, NEXP)
            for s in range(2):
                for i in range(NCLS):
                    a, c = PAIRS[i][s]
                    last = V.tensor_copy(hm[:, s, c, i:i + 1], hc[:, a, i:i + 1])
            last.then_inc(s_chm, 1)
            dve.wait_ge(s_cg, 1)
            link_up(V.tensor_tensor(lg[:], ps[0:NCLS, 1, 0:2 * NCLS].rearrange("p (i g) -> p i g", g=2),
                                    ident[0:NCLS, 0:NCLS][:, :, None].to_broadcast([NCLS, NCLS, 2]), ALU.mult))
            link_up(V.tensor_reduce(gt[:, 0:2], lg[:].rearrange("p i g -> p g i"), axis=AX.X, op=ALU.add))
            link_up(V.tensor_tensor(gt[:, 2:3], gt[:, 0:1], gt[:, 1:2], ALU.max))
            V.tensor_scalar(gt[:, 0:2], gt[:, 0:2], gt[:, 2:3], None, ALU.subtract).then_inc(s_cmax, 1)
            dve.wait_ge(s_cexp, 1)
            link_up(V.tensor_tensor(gt[:, 6:7], gt[:, 4:5], gt[:, 5:6], ALU.add))
            link_up(V.reciprocal(gt[:, 7:8], gt[:, 6:7]))
            link_up(V.tensor_scalar(gt[:, 4:6], gt[:, 4:6], gt[:, 7:8], None, ALU.mult))
            link_up(V.tensor_tensor(gt[:, 8:9], gt[:, 4:5], gt[:, 5:6], ALU.min))
            link_up(V.tensor_scalar(gt[:, 10:12], gt[:, 4:6], gt[:, 8:9], None, ALU.is_gt))
            link_up(V.tensor_tensor(gt[:, 10:12], gt[:, 10:12], gt[:, 4:6], ALU.mult))
            link_up(V.tensor_tensor(gt[:, 12:13], gt[:, 10:11], gt[:, 11:12], ALU.add))
            link_up(V.tensor_scalar(gt[:, 12:13], gt[:, 12:13], 1e-6, None, ALU.max))
            link_up(V.reciprocal(gt[:, 13:14], gt[:, 12:13]))
            link_up(V.tensor_scalar(gt[:, 14:16], gt[:, 10:12], gt[:, 13:14], None, ALU.mult))
            dve.wait_ge(s_cs, 1)
            dve.wait_ge(l_clsx, 16)
            link_up(V.scalar_tensor_tensor(co[:, 1, :], pair(1)[0:NCLS, :], gt[:, 14:15], co[:, 0, :],
                                           ALU.mult, ALU.add))
            V.scalar_tensor_tensor(co[:, 2, :], pair(2)[0:NCLS, :], gt[:, 15:16], co[:, 1, :],
                                   ALU.mult, ALU.add).then_inc(s_cout, 1)


def kernel(x, src, dst, L0_gnn_W, L0_gnn_attn_l, L0_gnn_attn_r, L0_gnn_W_res, L0_ffn_moe0_W1, L0_ffn_moe0_b1,
           L0_ffn_moe0_W2, L0_ffn_moe0_b2, L0_ffn_A1_W, L0_ffn_A1_b, L0_ffn_A2_W, L0_ffn_A2_b, L0_ffn_G_W,
           L0_ffn_mids):
    import concourse.bacc as bacc
    from concourse.bass_utils import run_bass_kernel_spmd

    def rows(a, n, fill):
        a = np.asarray(a)
        return np.concatenate([a, np.full((n - a.shape[0],) + a.shape[1:], fill, a.dtype)])

    def block_diagonal(w):
        out = np.zeros((P, P), w.dtype)
        for i in range(HC):
            out[i * DH:(i + 1) * DH, i * DH:(i + 1) * DH] = w.T
        return out

    src = rows(np.asarray(src, np.int32), EP, 0)
    dst = rows(np.asarray(dst, np.int32), EP, PAD_NODE)
    dst_next = np.concatenate([dst[1:], np.full(1, -1, np.int32)])
    edges = np.stack([src, dst, np.zeros(EP, np.int32), np.arange(EP, dtype=np.int32)], axis=1)
    w, w_res = np.asarray(L0_gnn_W), np.asarray(L0_gnn_W_res)
    attn = np.concatenate([np.asarray(L0_gnn_attn_l)[0].T, np.asarray(L0_gnn_attn_r)[0].T], axis=1)
    arrays = {
        "x": rows(x, NP, 0),
        "edges": edges.reshape(P, EC, 4),
        "src_b": src.reshape(EC, P).T,
        "dst_a": dst.reshape(P, EC),
        "dst_b": dst.reshape(EC, P).T,
        "dst_next": dst_next.reshape(P, EC),
        "dst_row": dst.reshape(1, EP),
        "dst_first": dst.reshape(P, EC)[:, 0].reshape(1, P),
        "dst_last": dst.reshape(P, EC)[:, EC - 1].reshape(1, P),
        "eye": np.eye(P, dtype=np.float32),
        "w_gnn": w,
        "w_gnn_bd": block_diagonal(w),
        "w_res_bd": block_diagonal(w_res),
        "attn": attn,
        "w1": L0_ffn_moe0_W1,
        "b1": L0_ffn_moe0_b1,
        "w2": L0_ffn_moe0_W2,
        "b2": L0_ffn_moe0_b2,
        "a1w": np.asarray(L0_ffn_A1_W).transpose(1, 0, 2),
        "a1b": np.asarray(L0_ffn_A1_b).T,
        "a2w": np.asarray(L0_ffn_A2_W).transpose(1, 0, 2),
        "a2b": L0_ffn_A2_b,
        "gw": np.asarray(L0_ffn_G_W).transpose(1, 0, 2).reshape(D, 2 * NCLS),
    }
    nc = bacc.Bacc("TRN2", target_bir_lowering=False, num_devices=1)
    sent, args = {}, []
    for name, a in arrays.items():
        a = np.ascontiguousarray(a)
        sent[f"in_{name}"] = a
        args.append(nc.dram_tensor(f"in_{name}", a.shape, mybir.dt.from_np(a.dtype), kind="ExternalInput").ap())
    args.append(nc.dram_tensor("out", (NP, D), mybir.dt.float32, kind="ExternalOutput").ap())
    gnn_ffn_kernel(nc, *args)
    r = run_bass_kernel_spmd(nc, [sent], core_ids=[0])
    return r.results[0]["out"][:N_NODES]
```

```python
import numpy as np
import concourse.bass as bass
from concourse import mybir
from contextlib import ExitStack

N_NODES = 50000
N_EDGES = 25000
D = 768
HEADS = 12
DH = D // HEADS
HID = 96
NCLS = 6
NEXP = 5
P = 128
NC = D // P
HC = P // DH

PAIR = 2
RING = 4
U = PAIR * RING
NT = -(-N_NODES // (P * U)) * U
NP = NT * P
EC = -(-N_EDGES // (P * RING)) * RING
EP = EC * P
PAD_NODE = NP - 1
NO_ROW = 1 << 20
BIG = 1e30
EPS = 1e-5
N_MEMSETS = 7
SLOPE = 0.2

GT0 = [[0, 1, 0, 0, 1, 0], [0, 1, 0, 0, 0, 1], [0, 0, 1, 0, 1, 0],
       [0, 0, 1, 0, 0, 1], [0, 0, 0, 1, 1, 0], [0, 0, 0, 1, 0, 1]]
PAIRS = [[(j - 1, k - 1) for j in range(1, 6) for k in range(1, 6) if j != k and g[j] and g[k]] for g in GT0]


def turns(eng, n, drain):
    yield 0
    yield 1
    with eng.Fori(2, n) as b:
        yield b
    for b in range(drain):
        yield n + b


def settle(eng):
    eng.nop(nofuse=True)


def exists(t, n):
    return not isinstance(t, int) or 0 <= t < n


def at_least(eng, sem, value):
    if not isinstance(value, int) or value > 0:
        eng.wait_ge(sem, value)


def gnn_ffn_kernel(nc, x, edges, dst_next, dst_a, dst_row, dst_first, dst_last,
                   eye, w_gnn, w_gnn_bd, w_res_bd, attn, w1, b1, w2, b2, a1w, a1b, a2w, a2b, gw, out):
    f32 = mybir.dt.float32
    f32r = mybir.dt.float32r
    i32 = mybir.dt.int32
    ALU = mybir.AluOpType
    ACT = mybir.ActivationFunctionType
    AX = mybir.AxisListType
    ds = bass.ds

    with ExitStack() as ctx:
        def sb(name, shape, dt=f32):
            return ctx.enter_context(nc.sbuf_tensor(name, shape, dt))

        def sem(name):
            return ctx.enter_context(nc.semaphore(name))

        sco_d = nc.dram_tensor("score_scratch", [HEADS, 2, EP], f32).ap()
        sta_d = nc.dram_tensor("stat_scratch", [4, EP], f32).ap()
        rec_d = nc.dram_tensor("rec_scratch", [EP, HEADS], f32).ap()
        agg_d = nc.dram_tensor("agg_scratch", [EP, D], f32).ap()
        row_d = nc.dram_tensor("row_scratch", [NP, 1], i32).ap()
        cls_d = nc.dram_tensor("cls_scratch", [NCLS, D], f32).ap()

        x_ring = sb("x_ring", [P, U, D])
        g_ring = sb("g_ring", [P, U, D])
        y_ring = sb("y_ring", [P, U, D])
        n12 = sb("n12", [P, 4, D])
        n1 = n12[:, 0:2, :]
        n2 = n12[:, 2:4, :]
        t1 = sb("t1", [P, 2, D])
        t2 = sb("t2", [P, 2, D])
        o_buf = sb("o_buf", [P, RING, D])

        ident = sb("ident", [P, P])
        wg_bd = sb("wg_bd", [P, P])
        wr_bd = sb("wr_bd", [P, P])
        w_dup = sb("w_dup", [DH, P])
        attn_sb = sb("attn_sb", [DH, 2 * HEADS])
        v_sb = sb("v_sb", [P, NC * (2 * HEADS + 2)])
        ones = sb("ones", [P, P])
        sv = sb("sv", [P, 2 * HEADS])
        w1_sb = sb("w1_sb", [P, NC, HID])
        b1_sb = sb("b1_sb", [HID, 1])
        w2_sb = sb("w2_sb", [HID + 1, D])
        w2_hi = sb("w2_hi", [HID + 1, D], f32r)
        w2_lo = sb("w2_lo", [HID + 1, D], f32r)
        h_sb = sb("h_sb", [HID, 2, P])
        h_hi = sb("h_hi", [HID + 1, 2, P], f32r)
        h_lo = sb("h_lo", [HID + 1, 2, P], f32r)
        half = sb("half", [P, 1])
        junk = sb("junk", [P, D])

        e_all = sb("e_all", [P, EC, 4], i32)
        e_slot = sb("e_slot", [P, RING, 4], i32)
        dsta = sb("dsta", [P, EC], i32)
        dstn = sb("dstn", [P, EC], i32)
        dstf = sb("dstf", [P, EC])
        dstbf = sb("dstbf", [P, EC])
        tmp_f = sb("tmp_f", [P, EC])
        last_f = sb("last_f", [P, EC])
        bn_a = sb("bn_a", [P, 2, 2, 2, 6])
        mv_a = sb("mv_a", [P, 2, 4])
        scores = sb("scores", [P, 2 * HEADS, EC])
        mv = sb("mv", [P, 4, EC])
        flat_t2 = t2[:, :, :].rearrange("p a b -> p (a b)")
        mve = flat_t2[:, 0:4 * EC].rearrange("p (n e) -> p n e", n=4)
        std = flat_t2[:, 4 * EC:6 * EC].rearrange("p (n e) -> p n e", n=2)
        sc_row = sb("sc_row", [HEADS, RING, 2 * P])
        rec = n12[:, :, :].rearrange("p a b -> p (a b)")[:, 0:EC * HEADS].rearrange("p (e h) -> p e h", h=HEADS)
        same = sb("same", [P, EC])
        same_n = sb("same_n", [P, EC])
        in_first = junk[:, 0:EC]
        in_last = junk[:, EC:2 * EC]
        pen = junk[:, 2 * EC:3 * EC]
        ends = sb("ends", [P, 2 * HEADS])
        carry_c = sb("carry_c", [P, 2 * HEADS])
        rowi = sb("rowi", [HEADS, 2, P], i32)
        rowf = sb("rowf", [HEADS, 2, P])
        link = sb("link", [HEADS, P + 1])
        whole = sb("whole", [HEADS, P])
        g_f = sb("g_f", [HEADS, P])
        g_b = sb("g_b", [HEADS, P])
        pens = sb("pens", [HEADS, 4, P])
        e_row = sb("e_row", [HEADS, 2, P])
        s_pad = sb("s_pad", [HEADS, P + 1])
        q_pad = sb("q_pad", [HEADS, P + 1])
        c_row = sb("c_row", [HEADS, 2, P])
        row_init = sb("row_init", [P, NT], i32)

        rec_b = sb("rec_b", [P, RING, HEADS])
        row_b = sb("row_b", [P, RING, P], i32)
        dst_slot = sb("dst_slot", [P, RING])
        same_m = sb("same_m", [P, 2, P])
        cont_m = sb("cont_m", [P, 2, P])

        nrow = sb("nrow", [P, U], i32)
        has = sb("has", [P, U])
        bn1 = sb("bn1", [P, 2, 2, 6])
        mv1 = sb("mv1", [P, U, 2])
        sum2 = sb("sum2", [P, U])
        nmean2 = sb("nmean2", [P, U])
        ssq2 = sb("ssq2", [P, U])
        ve1 = sb("ve1", [P, U])
        ve2 = sb("ve2", [P, U])
        r1 = sb("r1", [P, U])
        r2 = sb("r2", [P, U])
        nm1 = sb("nm1", [P, U])
        nm2 = sb("nm2", [P, U])

        cls_t = sb("cls_t", [P, NC, NCLS])
        gw_sb = sb("gw_sb", [P, NC, NCLS * 2])
        a1_sb = sb("a1_sb", [P, NC, NEXP, HID])
        a1b_sb = sb("a1b_sb", [HID, NEXP])
        a2_sb = sb("a2_sb", [HID + 1, NEXP, D])
        hc = sb("hc", [HID + 1, NEXP, NCLS])
        hm = sb("hm", [HID + 1, 2, NEXP, NCLS])
        lg = sb("lg", [NCLS, NCLS, 2])
        gt = sb("gt", [NCLS, 16])
        flat_scores = scores[:, :, :].rearrange("p a b -> p (a b)")
        co = flat_scores[0:NCLS, 0:3 * D].rearrange("p (a c) -> p a c", a=3)
        cls_x = flat_scores[0:NCLS // PAIR, 3 * D:(3 + PAIR) * D].rearrange("p (a c) -> p a c", a=PAIR)

        ps = ctx.enter_context(nc.psum_tensor("ps", [P, 8, 512], f32))

        def pair(n):
            return ps[:, 2 * n:2 * n + 2, :].rearrange("p a b -> p (a b)")[:, 0:D]

        l_const = sem("l_const")
        l_edges = sem("l_edges")
        s_memset = sem("s_memset")
        s_attn = sem("s_attn")
        s_v = sem("s_v")
        s_sv = sem("s_sv")
        s_dve = sem("s_dve")
        s_rowinit = sem("s_rowinit")
        d_rowinit = sem("d_rowinit")
        s_eslot = sem("s_eslot")
        d_gs = [sem(f"d_gs{u}") for u in range(RING)]
        d_gd = [sem(f"d_gd{u}") for u in range(RING)]
        d_scat = [sem(f"d_scat{u}") for u in range(RING)]
        s_tps = sem("s_tps")
        s_tpd = sem("s_tpd")
        s_tes = sem("s_tes")
        s_ted = sem("s_ted")
        s_scs = sem("s_scs")
        s_scd = sem("s_scd")
        s_bna = sem("s_bna")
        s_aga = sem("s_aga")
        s_keep = sem("s_keep")
        d_sco = [sem(f"d_sco{u}") for u in range(RING)]
        l_sco = sem("l_sco")
        s_va = sem("s_va")
        s_sqrt = sem("s_sqrt")
        s_rstd = sem("s_rstd")
        s_statt = sem("s_statt")
        s_staro = sem("s_staro")
        d_sta = sem("d_sta")
        l_sta = sem("l_sta")
        s_ends = sem("s_ends")
        s_endt = sem("s_endt")
        s_crow = sem("s_crow")
        s_ccol = sem("s_ccol")
        s_z = sem("s_z")
        s_exp = sem("s_exp")
        s_rec = sem("s_rec")
        d_rec = sem("d_rec")
        s_bslot = sem("s_bslot")
        d_xg = [sem(f"d_xg{u}") for u in range(RING)]
        d_rb = [sem(f"d_rb{u}") for u in range(RING)]
        s_msg = sem("s_msg")
        s_masks = sem("s_masks")
        s_sum = sem("s_sum")
        s_run = sem("s_run")
        s_wag = sem("s_wag")
        s_aggo = sem("s_aggo")
        d_agg = [sem(f"d_agg{u}") for u in range(RING)]
        d_x = [sem(f"d_x{u}") for u in range(RING)]
        d_nr = [sem(f"d_nr{u}") for u in range(RING)]
        d_g = [sem(f"d_g{u}") for u in range(RING)]
        d_out = [sem(f"d_out{u}") for u in range(2)]
        s_bn1 = sem("s_bn1")
        s_ag1 = sem("s_ag1")
        s_ve1 = sem("s_ve1")
        s_r1 = sem("s_r1")
        s_nm1 = sem("s_nm1")
        s_n1 = sem("s_n1")
        s_tp1 = sem("s_tp1")
        s_te1 = sem("s_te1")
        s_res = sem("s_res")
        s_has = sem("s_has")
        s_add = sem("s_add")
        s_y = sem("s_y")
        s_mean2 = sem("s_mean2")
        s_sq2 = sem("s_sq2")
        s_ve2 = sem("s_ve2")
        s_r2 = sem("s_r2")
        s_nm2 = sem("s_nm2")
        s_n2 = sem("s_n2")
        s_tp2 = sem("s_tp2")
        s_te2 = sem("s_te2")
        s_up = sem("s_up")
        s_h = sem("s_h")
        s_hhi = sem("s_hhi")
        s_hlo = sem("s_hlo")
        s_down = sem("s_down")
        s_o = sem("s_o")
        l_cls = sem("l_cls")
        s_clsx = sem("s_clsx")
        d_clsx = sem("d_clsx")
        l_clsx = sem("l_clsx")
        s_clst = sem("s_clst")
        s_ch = sem("s_ch")
        s_cg = sem("s_cg")
        s_chg = sem("s_chg")
        s_chm = sem("s_chm")
        s_cmax = sem("s_cmax")
        s_cexp = sem("s_cexp")
        s_cs = sem("s_cs")
        s_cout = sem("s_cout")
        d_cls = sem("d_cls")

        x_v = x.rearrange("(q p k) c -> q p k c", p=P, k=PAIR)
        out_v = out.rearrange("(q p k) c -> q p k c", p=P, k=PAIR)
        row_v = row_d.rearrange("(q p k) c -> q p (k c)", p=P, k=PAIR)
        rec_bv = rec_d.rearrange("(c p) r -> c p r", p=P)
        agg_v = agg_d.rearrange("(c p) d -> c p d", p=P)
        NCONST = 12
        VW = 2 * HEADS + 2
        OFF = 2 * HEADS
        fwd = x_ring[:, :, :].rearrange("p a b -> p (a b)")[:, 0:HEADS * EC].rearrange("p (h e) -> p h e", h=HEADS)
        bwd = x_ring[:, :, :].rearrange("p a b -> p (a b)")[:, HEADS * EC:2 * HEADS * EC]\
            .rearrange("p (h e) -> p h e", h=HEADS)
        work = g_ring[:, :, :].rearrange("p a b -> p (a b)")[:, 0:HEADS * EC].rearrange("p (h e) -> p h e", h=HEADS)

        stat_rows = y_ring[:, :, :].rearrange("p a b -> p (a b)")[0:EC // 2, 0:8 * P]\
            .rearrange("c (n i e) -> c n i e", n=4, i=2)

        block = ctx.enter_context(nc.Block())

        @block.sync
        def _(sp):
            sp.dma_start(ident[:], eye).then_inc(l_const, 16)
            sp.dma_start(w_dup[:, 0:DH], w_gnn).then_inc(l_const, 16)
            sp.dma_start(w_dup[:, DH:P], w_gnn).then_inc(l_const, 16)
            sp.dma_start(attn_sb[:], attn).then_inc(l_const, 16)
            sp.dma_start(wg_bd[:], w_gnn_bd).then_inc(l_const, 16)
            sp.dma_start(wr_bd[:], w_res_bd).then_inc(l_const, 16)
            sp.dma_start(w1_sb[:], w1.rearrange("(c p) h -> p c h", p=P)).then_inc(l_const, 16)
            sp.dma_start(b1_sb[:], b1.rearrange("(p a) -> p a", a=1)).then_inc(l_const, 16)
            sp.dma_start(w2_sb[0:HID, :], w2).then_inc(l_const, 16)
            sp.dma_start(w2_sb[HID:HID + 1, :], b2.rearrange("(a c) -> a c", a=1)).then_inc(l_const, 16)
            sp.dma_start(rowi[:, 0, :], dst_first.to_broadcast([HEADS, P])).then_inc(l_const, 16)
            sp.dma_start(rowi[:, 1, :], dst_last.to_broadcast([HEADS, P])).then_inc(l_const, 16)
            sp.dma_start(gw_sb[:], gw.rearrange("(c p) g -> p c g", p=P)).then_inc(l_cls, 16)
            sp.dma_start(a1_sb[:], a1w.rearrange("(c p) a h -> p c a h", p=P)).then_inc(l_cls, 16)
            sp.dma_start(a1b_sb[:], a1b).then_inc(l_cls, 16)
            sp.dma_start(a2_sb[0:HID, :, :], a2w).then_inc(l_cls, 16)
            sp.dma_start(a2_sb[HID:HID + 1, :, :], a2b.rearrange("(o a) d -> o a d", o=1)).then_inc(l_cls, 16)
            sp.wait_ge(s_rowinit, 1)
            sp.dma_start(row_d.rearrange("(p n) o -> p (n o)", p=P), row_init[:]).then_inc(d_rowinit, 16)
            for b in turns(sp, EC // RING, 0):
                for u in range(RING):
                    j = b * RING + u
                    sp.wait_ge(s_keep, j + 1)
                    sp.dma_start(sco_d[:, :, ds(j * P, P)],
                                 sc_row[:, u, :].rearrange("h (s e) -> h s e", s=2)).then_inc(d_sco[u], 16)
            for u in range(RING):
                sp.wait_ge(d_sco[u], 16 * (EC // RING))
            for side in range(2):
                sp.dma_start(scores[:, side * HEADS:(side + 1) * HEADS, :],
                             sco_d[:, side, :].rearrange("h (p e) -> p h e", p=P)).then_inc(l_sco, 16)
            for n in range(4):
                sp.wait_ge(s_staro, n + 1)
                sp.dma_start(sta_d[n].rearrange("(i c e) -> c i e", i=2, e=P), stat_rows[:, n, :, :]).then_inc(d_sta, 16)
            sp.wait_ge(d_sta, 64)
            sp.dma_start(mve[:], sta_d.rearrange("n (p e) -> p n e", p=P)).then_inc(l_sta, 16)
            sp.wait_ge(s_rec, 1)
            sp.dma_start(rec_d.rearrange("(p e) r -> p e r", p=P), rec[:]).then_inc(d_rec, 16)
            sp.wait_ge(d_rec, 16)
            for b in turns(sp, EC // RING, 1):
                for u in range(RING):
                    c = b * RING + u
                    if exists(c, EC):
                        at_least(sp, s_sum, c - RING + 2)
                        sp.dma_start(rec_b[:, u, :], rec_bv[ds(c, 1)].rearrange("a p r -> p (a r)"))\
                            .then_inc(d_rb[u], 16)
                        sp.dma_start(row_b[:, u, :], dst_row[0:1, ds(c * P, P)].to_broadcast([P, P]))\
                            .then_inc(d_rb[u], 16)
                    cs = c - RING
                    if exists(cs, EC):
                        sp.wait_ge(s_aggo, cs + 1)
                        sp.dma_start(agg_v[ds(cs, 1)].rearrange("a p d -> p (a d)"), o_buf[:, u, :])\
                            .then_inc(d_agg[u], 16)
            for u in range(RING):
                sp.wait_ge(d_agg[u], 16 * (EC // RING))
            for u in range(RING):
                sp.wait_ge(d_scat[u], 16 * (EC // RING))
            for b in turns(sp, NT // U, 2):
                for u in range(U):
                    t = b * U + u
                    if u % PAIR == 0 and exists(t, NT):
                        j = u // PAIR
                        at_least(sp, s_y, t - U + PAIR)
                        at_least(sp, s_has, t - U + PAIR)
                        at_least(sp, s_n1, t - U + PAIR)
                        sp.dma_start(x_ring[:, u:u + PAIR, :],
                                     x_v[ds(b * RING + j, 1)].rearrange("q p k c -> p (q k) c")).then_inc(d_x[j], 16)
                        at_least(sp, d_g[j], 32 * b)
                        sp.dma_start(nrow[:, u:u + PAIR],
                                     row_v[ds(b * RING + j, 1)].rearrange("q p k -> p (q k)")).then_inc(d_nr[j], 16)
                    to = t - 13
                    if (u - 13) % PAIR == 1 and exists(to, NT):
                        v = (u - 13) % U // PAIR
                        sp.wait_ge(s_o, to + 1)
                        s = v % 2
                        first = isinstance(b, int) and to == 1
                        lo = NCLS // PAIR if first else 0
                        pair_no = (to - 1) // PAIR if isinstance(b, int) else b * RING + (u - 14) // PAIR
                        sp.dma_start(out_v[ds(pair_no, 1), lo:P].rearrange("q p k c -> p (q k) c"),
                                     o_buf[lo:P, PAIR * s:PAIR * s + PAIR, :]).then_inc(d_out[s], 16)
            sp.wait_ge(s_clsx, PAIR)
            sp.dma_start(cls_d.rearrange("(p k) c -> p k c", k=PAIR), cls_x).then_inc(d_clsx, 16)
            sp.wait_ge(d_clsx, 16)
            sp.dma_start(co[:, 0, :], cls_d).then_inc(l_clsx, 16)
            for s in range(2):
                sp.wait_ge(d_out[s], 16 * (NT // U) * 2)
            sp.wait_ge(s_cout, 1)
            sp.dma_start(out[0:NCLS, :], co[:, 2, :]).then_inc(d_cls, 16)
            sp.wait_ge(d_cls, 16)

        @block.gpsimd
        def _(pool):
            pool.wait_ge(d_rowinit, 16)
            for b in turns(pool, EC // RING, 0):
                for u in range(RING):
                    j = b * RING + u
                    pool.wait_ge(s_eslot, j + 1)
                    at_least(pool, s_tpd, j - RING + 1)
                    at_least(pool, s_aga, j - RING + 1)
                    settle(pool)
                    pool.indirect_dma_start(g_ring[:, u, :], None, x,
                                            bass.IndirectOffsetOnAxis(e_slot[:, u, 0:1], 0)).then_inc(d_gs[u], 16)
                    pool.indirect_dma_start(g_ring[:, RING + u, :], None, x,
                                            bass.IndirectOffsetOnAxis(e_slot[:, u, 1:2], 0)).then_inc(d_gd[u], 16)
                    pool.indirect_dma_start(row_d, bass.IndirectOffsetOnAxis(e_slot[:, u, 2:3], 0),
                                            e_slot[:, u, 3:4], None, bounds_check=NP - 1, oob_is_err=False)\
                        .then_inc(d_scat[u], 16)
            pool.wait_ge(s_rec, 1)
            for b in turns(pool, EC // RING, 1):
                for u in range(RING):
                    c = b * RING + u
                    if exists(c, EC):
                        pool.wait_ge(s_bslot, c + 1)
                        at_least(pool, s_msg, c - RING + 1)
                        settle(pool)
                        pool.indirect_dma_start(g_ring[:, u, :], None, x,
                                                bass.IndirectOffsetOnAxis(e_slot[:, u, 0:1], 0)).then_inc(d_xg[u], 16)
                    cm = c - 1
                    if exists(cm, EC):
                        v = (u - 1) % RING
                        w = v % 2
                        pool.wait_ge(d_rb[v], 32 * (b + 1 if u >= 1 else b))
                        at_least(pool, s_sum, cm - 1)
                        at_least(pool, s_run, cm - 1)
                        settle(pool)
                        pool.tensor_scalar(same_m[:, w, :], row_b[:, v, :], dst_slot[:, v:v + 1], None, ALU.is_equal)
                        if isinstance(cm, int) and cm == 0:
                            pool.memset(cont_m[:, w, :], 0.0).then_inc(s_masks, 1)
                        else:
                            pool.tensor_scalar(cont_m[:, w, :], row_b[:, v, :], row_b[:, (v - 1) % RING, P - 1:P], None,
                                               ALU.is_equal).then_inc(s_masks, 1)
            for u in range(RING):
                pool.wait_ge(d_agg[u], 16 * (EC // RING))
            pool.wait_ge(s_msg, EC)
            for b in turns(pool, NT // U, 2):
                for u in range(U):
                    t = b * U + u
                    if u % PAIR == 0 and exists(t, NT):
                        j = u // PAIR
                        pool.wait_ge(d_nr[j], 16 * b + 16)
                        at_least(pool, s_add, t - U + PAIR)
                        for k in range(PAIR):
                            settle(pool)
                            pool.indirect_dma_start(g_ring[:, u + k, :], None, agg_d,
                                                    bass.IndirectOffsetOnAxis(nrow[:, u + k:u + k + 1], 0),
                                                    bounds_check=EP - 1, oob_is_err=False).then_inc(d_g[j], 16)
                    tp = t - 5
                    if exists(tp, NT):
                        v = (u - 5) % U
                        pool.wait_ge(s_ve2, tp + 1)
                        pool.tensor_tensor(r2[:, v:v + 1], ve2[:, v:v + 1], half[:], ALU.pow).then_inc(s_r2, 1)
                    ty = t - 6
                    if exists(ty, NT):
                        v = (u - 6) % U
                        pool.wait_ge(s_nm2, ty + 1)
                        at_least(pool, s_tp2, ty - 1)
                        settle(pool)
                        pool.tensor_scalar(n2[:, v % 2, :], y_ring[:, v, :], r2[:, v:v + 1], nm2[:, v:v + 1],
                                           ALU.mult, ALU.add).then_inc(s_n2, 1)
                    tn = t - 1
                    if exists(tn, NT):
                        v = (u - 1) % U
                        pool.wait_ge(s_nm1, tn + 1)
                        at_least(pool, s_tp1, tn - 1)
                        settle(pool)
                        pool.tensor_scalar(n1[:, v % 2, :], x_ring[:, v, :], r1[:, v:v + 1], nm1[:, v:v + 1],
                                           ALU.mult, ALU.add).then_inc(s_n1, 1)
                    if exists(t, NT):
                        pool.wait_ge(s_ve1, t + 1)
                        pool.tensor_tensor(r1[:, u:u + 1], ve1[:, u:u + 1], half[:], ALU.pow).then_inc(s_r1, 1)

        @block.scalar
        def _(act):
            act.dma_start(e_all[:], edges).then_inc(l_edges, 16)
            act.dma_start(dsta[:], dst_a).then_inc(l_edges, 16)
            act.dma_start(dstn[:], dst_next).then_inc(l_edges, 16)
            for b in turns(act, EC // RING, 1):
                for u in range(RING):
                    j = b * RING + u
                    if exists(j, EC):
                        act.wait_ge(s_tps, j + 1)
                        at_least(act, s_scs, j)
                        nc.scalar.activation(t1[:, 0, :], pair(0), ACT.Copy).then_inc(s_tes, 1)
                        act.wait_ge(s_tpd, j + 1)
                        at_least(act, s_scd, j)
                        nc.scalar.activation(t1[:, 1, :], pair(1), ACT.Copy).then_inc(s_ted, 1)
            act.wait_ge(s_va, 1)
            nc.scalar.activation(std[:], mv[:, 1:4:2, :], ACT.Sqrt).then_inc(s_sqrt, 1)
            act.wait_ge(s_z, 1)
            nc.scalar.activation(scores[:, 0:HEADS, :], fwd, ACT.Exp).then_inc(s_exp, 1)
            for b in turns(act, EC // RING, 0):
                for u in range(RING):
                    c = b * RING + u
                    act.wait_ge(s_wag, c + 1)
                    at_least(act, d_agg[u], 16 * b)
                    nc.scalar.activation(o_buf[:, u, :], pair(2 + u % 2), ACT.Copy).then_inc(s_aggo, 1)
            for b in turns(act, NT // U, 2):
                for u in range(U):
                    t = b * U + u
                    ta = t - 2
                    if exists(ta, NT):
                        act.wait_ge(s_tp1, ta + 1)
                        at_least(act, s_res, ta - 1)
                        nc.scalar.activation(t1[:, u % 2, :], pair(0), ACT.Copy).then_inc(s_te1, 1)
                    tq = t - 4
                    if exists(tq, NT):
                        v = (u - 4) % U
                        act.wait_ge(s_mean2, tq + 1)
                        at_least(act, s_sq2, tq)
                        nc.scalar.activation(junk[:], y_ring[:, v, :], ACT.Square, bias=nmean2[:, v:v + 1],
                                             accum_out=ssq2[:, v:v + 1]).then_inc(s_sq2, 1)
                    tb = t - 7
                    if exists(tb, NT):
                        act.wait_ge(s_tp2, tb + 1)
                        at_least(act, s_up, tb - 1)
                        nc.scalar.activation(t2[:, (u - 7) % 2, :], pair(0), ACT.Copy).then_inc(s_te2, 1)
                        if isinstance(b, int) and tb < PAIR:
                            act.wait_ge(s_te2, tb + 1)
                            nc.scalar.activation(cls_t[:, :, tb:NCLS:PAIR],
                                                 t2[:, (u - 7) % 2, :].rearrange("p (c n) -> p c n", c=NC)
                                                 [:, :, 0:NCLS // PAIR], ACT.Copy).then_inc(s_clst, 1)
                    th = t - 8
                    if exists(th, NT):
                        v = (u - 8) % 2
                        act.wait_ge(s_up, th + 1)
                        at_least(act, s_hlo, th - 1)
                        nc.scalar.activation(h_sb[:, v, :], ps[0:HID, 6 + v, 0:P], ACT.Gelu, bias=b1_sb[:])\
                            .then_inc(s_h, 1)
                        act.wait_ge(s_h, th + 1)
                        at_least(act, s_down, th - 1)
                        nc.scalar.activation(h_hi[0:HID, v, :], h_sb[:, v, :], ACT.Copy).then_inc(s_hhi, 1)
            act.wait_ge(l_cls, 16 * 5)
            act.wait_ge(s_ch, 1)
            for a in range(NEXP):
                nc.scalar.activation(hc[0:HID, a, :], ps[0:HID, 0, a * NCLS:(a + 1) * NCLS], ACT.Gelu,
                                     bias=a1b_sb[:, a:a + 1]).then_inc(s_chg, 1)
            act.wait_ge(s_cmax, 1)
            nc.scalar.activation(gt[:, 4:6], gt[:, 0:2], ACT.Exp).then_inc(s_cexp, 1)

        @block.tensor
        def _(pe):
            pe.wait_ge(l_const, 16 * NCONST)
            pe.wait_ge(s_memset, N_MEMSETS)
            nc.tensor.matmul(ps[:, 0, 0:2 * HEADS], w_dup[:], attn_sb[:], start=True, stop=True).then_inc(s_attn, 1)
            pe.wait_ge(s_v, 4)
            for c in range(NC):
                last = nc.tensor.matmul(ps[:, 1, 0:2 * HEADS], ones[:], v_sb[:, OFF * c:OFF * c + OFF],
                                        start=(c == 0), stop=(c == NC - 1))
            last.then_inc(s_sv, 1)
            pe.wait_ge(s_v, 5)

            def transposes(dst, src, done):
                for c in range(NC):
                    last = nc.tensor.transpose(dst[:, c * P:(c + 1) * P], src[:, c * P:(c + 1) * P], ident[:])
                last.then_inc(done, 1)

            def score(dst, src, off, done):
                for c in range(NC):
                    last = nc.tensor.matmul(dst, v_sb[:, OFF * c + off:OFF * c + off + HEADS],
                                            src[:, c * P:(c + 1) * P], start=(c == 0), stop=(c == NC - 1))
                last.then_inc(done, 1)

            for b in turns(pe, EC // RING, 1):
                for u in range(RING):
                    j = b * RING + u
                    if exists(j, EC):
                        pe.wait_ge(d_gs[u], 16 * b + 16)
                        at_least(pe, s_tes, j)
                        transposes(pair(0), g_ring[:, u, :], s_tps)
                    jd = j - 1
                    if exists(jd, EC):
                        pe.wait_ge(s_ted, jd + 1)
                        score(ps[0:HEADS, 4 + (u - 1) % 2, P:2 * P], t1[:, 1, :], HEADS, s_scd)
                    if exists(j, EC):
                        pe.wait_ge(d_gd[u], 16 * b + 16)
                        at_least(pe, s_ted, j)
                        transposes(pair(1), g_ring[:, RING + u, :], s_tpd)
                        pe.wait_ge(s_tes, j + 1)
                        at_least(pe, s_keep, j - 1)
                        score(ps[0:HEADS, 4 + u % 2, 0:P], t1[:, 0, :], 0, s_scs)
            pe.wait_ge(s_rstd, 1)
            for n in range(4):
                at_least(pe, s_staro, n - 1)
                for i in range(2):
                    last = nc.tensor.transpose(ps[0:EC // 2, n % 2, i * P:(i + 1) * P],
                                               mv[:, n, i * (EC // 2):(i + 1) * (EC // 2)], ident[:])
                last.then_inc(s_statt, 1)
            for n in range(2):
                pe.wait_ge(s_ends, n + 1)
                for i in range(2):
                    last = nc.tensor.transpose(ps[0:HEADS, 6, i * P:(i + 1) * P],
                                               ends[:, i * HEADS:(i + 1) * HEADS], ident[:])
                last.then_inc(s_endt, 1)
                pe.wait_ge(s_crow, n + 1)
                for i in range(2):
                    last = nc.tensor.transpose(ps[:, 7, i * HEADS:(i + 1) * HEADS], c_row[:, i, :],
                                               ident[0:HEADS, 0:HEADS])
                last.then_inc(s_ccol, 1)
            for b in turns(pe, EC // RING, 1):
                for u in range(RING):
                    c = b * RING + u
                    if exists(c, EC):
                        pe.wait_ge(s_msg, c + 1)
                        pe.wait_ge(s_masks, c + 1)
                        at_least(pe, s_run, c - 1)
                        for i in range(NC):
                            last = nc.tensor.matmul(pair(u % 2)[:, i * P:(i + 1) * P],
                                                    y_ring[:, u % 2, i * P:(i + 1) * P], same_m[:, u % 2, :],
                                                    start=True, stop=True)
                        last.then_inc(s_sum, 1)
                    cw = c - 1
                    if exists(cw, EC):
                        v = (u - 1) % 2
                        pe.wait_ge(s_run, cw + 1)
                        at_least(pe, s_aggo, cw - 1)
                        for i in range(NC):
                            last = nc.tensor.matmul(pair(2 + v)[:, i * P:(i + 1) * P],
                                                    y_ring[:, 2 + v, i * P:(i + 1) * P], wg_bd[:],
                                                    start=True, stop=True)
                        last.then_inc(s_wag, 1)
            pe.wait_ge(s_aggo, EC)
            pe.wait_ge(s_memset, N_MEMSETS)
            for b in turns(pe, NT // U, 2):
                for u in range(U):
                    t = b * U + u
                    ta = t - 2
                    if exists(ta, NT):
                        pe.wait_ge(s_n1, ta + 1)
                        at_least(pe, s_te2, t - 7)
                        if isinstance(b, int) and b == 0:
                            at_least(pe, s_te1, ta)
                        transposes(pair(0), n1[:, u % 2, :], s_tp1)
                    tr = t - 3
                    if exists(tr, NT):
                        pe.wait_ge(s_te1, tr + 1)
                        at_least(pe, s_add, tr)
                        for i in range(NC):
                            last = nc.tensor.matmul(pair(1)[:, i * P:(i + 1) * P],
                                                    t1[:, (u - 3) % 2, i * P:(i + 1) * P], wr_bd[:],
                                                    start=True, stop=True)
                        last.then_inc(s_res, 1)
                    tb = t - 7
                    if exists(tb, NT):
                        pe.wait_ge(s_n2, tb + 1)
                        if exists(ta, NT):
                            pe.wait_ge(s_te1, ta + 1)
                        else:
                            pe.wait_ge(s_te2, tb)
                        transposes(pair(0), n2[:, (u - 7) % 2, :], s_tp2)
                    tu = t - 8
                    if exists(tu, NT):
                        v = (u - 8) % 2
                        pe.wait_ge(s_te2, tu + 1)
                        at_least(pe, s_h, tu - 1)
                        for i in range(NC):
                            last = nc.tensor.matmul(ps[0:HID, 6 + v, 0:P], w1_sb[:, i, :],
                                                    t2[:, v, i * P:(i + 1) * P],
                                                    start=(i == 0), stop=(i == NC - 1))
                        last.then_inc(s_up, 1)
                    td = t - 9
                    if exists(td, NT):
                        v = (u - 9) % 2
                        pe.wait_ge(s_hlo, td + 1)
                        at_least(pe, s_o, td)
                        for lo, hi in ((0, 512), (512, D)):
                            for n, (h, w) in enumerate(((h_hi, w2_hi), (h_hi, w2_lo), (h_lo, w2_hi))):
                                last = nc.tensor.matmul(pair(2)[:, lo:hi], h[:, v, :], w[:, lo:hi],
                                                        start=(n == 0), stop=(n == 2))
                        last.then_inc(s_down, 1)
            pe.wait_ge(s_te2, NT)
            pe.wait_ge(l_cls, 16 * 5)
            pe.wait_ge(s_clst, PAIR)
            for a in range(NEXP):
                for i in range(NC):
                    last = nc.tensor.matmul(ps[0:HID, 0, a * NCLS:(a + 1) * NCLS], a1_sb[:, i, a, :], cls_t[:, i, :],
                                            start=(i == 0), stop=(i == NC - 1))
            last.then_inc(s_ch, 1)
            for i in range(NC):
                last = nc.tensor.matmul(ps[0:NCLS, 1, 0:2 * NCLS], cls_t[:, i, :], gw_sb[:, i, :],
                                        start=(i == 0), stop=(i == NC - 1))
            last.then_inc(s_cg, 1)
            pe.wait_ge(s_chm, 1)
            pe.wait_ge(s_o, NT)
            for s in range(2):
                for lo, hi in ((0, 512), (512, D)):
                    for a in range(NEXP):
                        last = nc.tensor.matmul(pair(1 + s)[0:NCLS, lo:hi], hm[:, s, a, :], a2_sb[:, a, lo:hi],
                                                start=(a == 0), stop=(a == NEXP - 1))
            last.then_inc(s_cs, 1)

        @block.vector
        def _(dve):
            done = [0]

            def link_up(ins):
                done[0] += 1
                ins.then_inc(s_dve, 1)
                dve.wait_ge(s_dve, done[0])

            V = nc.vector
            V.memset(ones[:], 1.0).then_inc(s_memset, 1)
            V.memset(v_sb[:], 0.0).then_inc(s_memset, 1)
            V.memset(half[:], -0.5).then_inc(s_memset, 1)
            V.memset(h_hi[HID:HID + 1, :, :].bitcast(f32), 1.0).then_inc(s_memset, 1)
            V.memset(h_lo[HID:HID + 1, :, :].bitcast(f32), 0.0).then_inc(s_memset, 1)
            V.memset(row_init[:], NO_ROW).then_inc(s_rowinit, 1)
            V.memset(hc[HID:HID + 1, :, :], 1.0).then_inc(s_memset, 1)
            V.memset(hm[:], 0.0).then_inc(s_memset, 1)
            dve.wait_ge(s_memset, N_MEMSETS)
            dve.wait_ge(l_const, 16 * NCONST)
            dve.wait_ge(s_attn, 1)
            v26 = v_sb[:, :].rearrange("p (c w) -> p c w", w=VW)
            for par in range(HC):
                rows = slice(par * DH, (par + 1) * DH)
                for side in range(2):
                    V.tensor_copy(v26[rows, :, side * HEADS + par],
                                  ps[rows, 0, side * HEADS + par:(side + 1) * HEADS:HC]).then_inc(s_v, 1)
            dve.wait_ge(s_sv, 1)
            V.tensor_copy(sv[:], ps[:, 1, 0:2 * HEADS]).then_inc(s_v, 1)
            link_up(V.tensor_copy(w2_hi[:], w2_sb[:]))
            link_up(V.tensor_tensor(w2_lo[:], w2_sb[:], w2_hi[:].bitcast(f32), ALU.subtract))
            dve.wait_ge(l_edges, 16 * 3)
            link_up(V.tensor_copy(dstf[:], dsta[:]))
            link_up(V.tensor_copy(dstbf[:], e_all[:, :, 1]))
            link_up(V.tensor_copy(tmp_f[:], dstn[:]))
            link_up(V.tensor_tensor(last_f[:], dstbf[:], tmp_f[:], ALU.is_equal))
            link_up(V.scalar_tensor_tensor(tmp_f[:], last_f[:], float(NO_ROW), dstbf[:], ALU.mult, ALU.add))
            link_up(V.tensor_copy(e_all[:, :, 2], tmp_f[:]))
            for b in turns(dve, EC // RING, 1):
                for u in range(RING):
                    j = b * RING + u
                    if exists(j, EC):
                        at_least(dve, d_gs[u], 16 * b)
                        at_least(dve, d_gd[u], 16 * b)
                        at_least(dve, d_scat[u], 16 * b)
                        V.tensor_copy(e_slot[:, u, :], e_all[:, ds(j, 1), :].rearrange("p a b -> p (a b)"))\
                            .then_inc(s_eslot, 1)
                    jb = j - 2
                    if exists(jb, EC):
                        v = (u - 2) % RING
                        w = v % 2
                        n = (b * 16 + 16) if u >= 2 else (b * 16)
                        dve.wait_ge(d_gs[v], n)
                        dve.wait_ge(d_gd[v], n)
                        for side in range(2):
                            for h in range(2):
                                V.bn_stats(bn_a[:, w, side, h, :],
                                           g_ring[:, side * RING + v, h * (D // 2):(h + 1) * (D // 2)]).then_inc(s_bna, 1)
                        dve.wait_ge(s_bna, jb * 4 + 4)
                        for side in range(2):
                            settle(dve)
                            last = V.bn_aggr(mv_a[:, w, 2 * side:2 * side + 2],
                                             bn_a[:, w, side, :, :].rearrange("p a b -> p (a b)"))
                        last.then_inc(s_aga, 1)
                        dve.wait_ge(s_aga, jb + 1)
                        V.tensor_copy(mv[:, :, ds(jb, 1)].rearrange("p a b -> p (a b)"), mv_a[:, w, :])
                    jk = j - 3
                    if exists(jk, EC):
                        w = (u - 3) % 2
                        dve.wait_ge(s_scs, jk + 1)
                        dve.wait_ge(s_scd, jk + 1)
                        v = (u - 3) % RING
                        at_least(dve, d_sco[v], 16 * (b if u >= 3 else b - 1))
                        V.tensor_copy(sc_row[:, v, :], ps[0:HEADS, 4 + w, 0:2 * P]).then_inc(s_keep, 1)
            dve.wait_ge(s_keep, EC)
            V.tensor_scalar(mv[:, 1:4:2, :], mv[:, 1:4:2, :], EPS, None, ALU.add).then_inc(s_va, 1)
            dve.wait_ge(s_sqrt, 1)
            link_up(V.reciprocal(std[:], std[:]))
            tmp2 = fwd[:, 0:2, :]
            link_up(V.tensor_tensor(tmp2, std[:], std[:], ALU.mult))
            link_up(V.tensor_tensor(tmp2, tmp2, mv[:, 1:4:2, :], ALU.mult))
            link_up(V.tensor_scalar(tmp2, tmp2, -0.5, 1.5, ALU.mult, ALU.add))
            V.tensor_tensor(mv[:, 1:4:2, :], std[:], tmp2, ALU.mult).then_inc(s_rstd, 1)
            for n in range(4):
                dve.wait_ge(s_statt, n + 1)
                V.tensor_copy(stat_rows[:, n, :, :].rearrange("c i e -> c (i e)"), ps[0:EC // 2, n % 2, 0:2 * P])\
                    .then_inc(s_staro, 1)
            link_up(V.memset(same[:, 0:1], 0.0))
            link_up(V.tensor_tensor(same[:, 1:EC], dstf[:, 1:EC], dstf[:, 0:EC - 1], ALU.is_equal))
            link_up(V.memset(same_n[:, EC - 1:EC], 0.0))
            link_up(V.tensor_copy(same_n[:, 0:EC - 1], same[:, 1:EC]))
            link_up(V.tensor_scalar(in_first[:], dstf[:], dstf[:, 0:1], None, ALU.is_equal))
            link_up(V.tensor_scalar(in_last[:], dstf[:], dstf[:, EC - 1:EC], None, ALU.is_equal))
            link_up(V.tensor_copy(rowf[:], rowi[:]))
            link_up(V.memset(link[:], 0.0))
            link_up(V.tensor_tensor(link[:, 1:P], rowf[:, 0, 1:P], rowf[:, 1, 0:P - 1], ALU.is_equal))
            link_up(V.tensor_tensor(whole[:], rowf[:, 0, :], rowf[:, 1, :], ALU.is_equal))
            link_up(V.tensor_tensor(g_f[:], whole[:], link[:, 0:P], ALU.mult))
            link_up(V.tensor_tensor(g_b[:], whole[:], link[:, 1:P + 1], ALU.mult))
            for n, m in enumerate((g_f[:], g_b[:], link[:, 0:P], link[:, 1:P + 1])):
                link_up(V.tensor_scalar(pens[:, n, :], m, 1.0, BIG, ALU.subtract, ALU.mult))
            link_up(V.memset(s_pad[:], 0.0))
            link_up(V.memset(q_pad[:], 0.0))
            dve.wait_ge(l_sco, 32)
            dve.wait_ge(l_sta, 16)
            dve.wait_ge(s_v, 5)

            def per_edge(row):
                return row[:, None, :].to_broadcast([P, HEADS, EC])

            def per_head(col):
                return col[:, :, None].to_broadcast([P, HEADS, EC])

            for n in range(2):
                part = scores[:, n * HEADS:(n + 1) * HEADS, :]
                link_up(V.tensor_tensor(fwd, per_edge(mve[:, 2 * n, :]), per_head(sv[:, n * HEADS:(n + 1) * HEADS]),
                                        ALU.mult))
                link_up(V.tensor_tensor(part, part, fwd, ALU.subtract))
                link_up(V.tensor_tensor(part, part, per_edge(mve[:, 2 * n + 1, :]), ALU.mult))
            e_v = scores[:, 0:HEADS, :]
            a2_v = scores[:, HEADS:2 * HEADS, :]
            link_up(V.tensor_tensor(fwd, e_v, a2_v, ALU.add))
            link_up(V.scalar_tensor_tensor(e_v.rearrange("p h e -> p (h e)"), fwd.rearrange("p h e -> p (h e)"), SLOPE,
                                           fwd.rearrange("p h e -> p (h e)"), ALU.mult, ALU.max))

            def scan(out_, d0, d1, init, op0, op1):
                for h in range(HEADS):
                    last = V.tensor_tensor_scan(out_(h), d0, d1(h), init, op0, op1)
                link_up(last)

            def carries(n, g0, g1, ops):
                link_up(V.tensor_copy(ends[:, 0:HEADS], fwd[:, :, EC - 1]))
                V.tensor_copy(ends[:, HEADS:2 * HEADS], bwd[:, :, 0]).then_inc(s_ends, 1)
                dve.wait_ge(s_endt, n + 1)
                link_up(V.tensor_copy(e_row[:].rearrange("h a b -> h (a b)"), ps[0:HEADS, 6, 0:2 * P]))
                link_up(V.tensor_tensor_scan(s_pad[:, 1:P + 1], g0, e_row[:, 0, :], 0.0, *ops))
                link_up(V.tensor_tensor_scan(q_pad[:, 0:P][:, ::-1], g1[:, ::-1],
                                             e_row[:, 1, ::-1], 0.0, *ops))

            link_up(V.tensor_scalar(pen[:], same[:], 1.0, BIG, ALU.subtract, ALU.mult))
            scan(lambda h: fwd[:, h, :], pen[:], lambda h: e_v[:, h, :], -BIG, ALU.add, ALU.max)
            link_up(V.tensor_scalar(pen[:], same_n[:], 1.0, BIG, ALU.subtract, ALU.mult))
            scan(lambda h: bwd[:, h, ::-1], pen[:, ::-1], lambda h: fwd[:, h, ::-1], -BIG, ALU.add, ALU.max)
            carries(0, pens[:, 0, :], pens[:, 1, :], (ALU.add, ALU.max))
            link_up(V.tensor_tensor(c_row[:, 0, :], s_pad[:, 0:P], pens[:, 2, :], ALU.add))
            V.tensor_tensor(c_row[:, 1, :], q_pad[:, 1:P + 1], pens[:, 3, :], ALU.add).then_inc(s_crow, 1)
            dve.wait_ge(s_ccol, 1)
            link_up(V.tensor_copy(carry_c[:], ps[:, 7, 0:2 * HEADS]))
            for side, inside in enumerate((in_first, in_last)):
                link_up(V.tensor_scalar(pen[:], inside[:], 1.0, BIG, ALU.subtract, ALU.mult))
                link_up(V.tensor_tensor(work, per_head(carry_c[:, side * HEADS:(side + 1) * HEADS]), per_edge(pen[:]),
                                        ALU.add))
                link_up(V.tensor_tensor(bwd, bwd, work, ALU.max))
            V.tensor_tensor(fwd, e_v, bwd, ALU.subtract).then_inc(s_z, 1)
            dve.wait_ge(s_exp, 1)
            scan(lambda h: fwd[:, h, :], same[:], lambda h: e_v[:, h, :], 0.0, ALU.mult, ALU.add)
            scan(lambda h: bwd[:, h, ::-1], same_n[:, ::-1], lambda h: fwd[:, h, ::-1], 0.0, ALU.mult, ALU.max)
            carries(1, g_f[:], g_b[:], (ALU.mult, ALU.add))
            link_up(V.tensor_tensor(c_row[:, 0, :], s_pad[:, 0:P], link[:, 0:P], ALU.mult))
            V.tensor_tensor(c_row[:, 1, :], q_pad[:, 1:P + 1], link[:, 1:P + 1], ALU.mult).then_inc(s_crow, 1)
            dve.wait_ge(s_ccol, 2)
            link_up(V.tensor_copy(carry_c[:], ps[:, 7, 0:2 * HEADS]))
            for side, inside in enumerate((in_first, in_last)):
                link_up(V.tensor_tensor(work, per_head(carry_c[:, side * HEADS:(side + 1) * HEADS]),
                                        per_edge(inside[:]), ALU.mult))
                link_up(V.tensor_tensor(bwd, bwd, work, ALU.add))
            link_up(V.tensor_scalar(bwd, bwd, 1e-16, None, ALU.max))
            link_up(V.reciprocal(fwd, bwd))
            link_up(V.tensor_tensor(fwd, fwd, per_edge(mve[:, 1, :]), ALU.mult))
            V.tensor_tensor(rec[:].rearrange("p e h -> p h e"), fwd, e_v, ALU.mult).then_inc(s_rec, 1)
            for u in range(RING):
                dve.wait_ge(d_scat[u], 16 * (EC // RING))
            for b in turns(dve, EC // RING, 1):
                for u in range(RING):
                    c = b * RING + u
                    if exists(c, EC):
                        at_least(dve, d_xg[u], 16 * b)
                        at_least(dve, s_masks, c - RING + 1)
                        V.tensor_copy(dst_slot[:, u:u + 1], dstbf[:, ds(c, 1)])
                        V.tensor_copy(e_slot[:, u, 0:1], e_all[:, ds(c, 1), 0]).then_inc(s_bslot, 1)
                    cm = c - 2
                    if exists(cm, EC):
                        v = (u - 2) % RING
                        w = v % 2
                        n = b + 1 if u >= 2 else b
                        dve.wait_ge(d_xg[v], n * 16)
                        dve.wait_ge(d_rb[v], n * 32)
                        at_least(dve, s_sum, cm - 1)
                        V.scalar_tensor_tensor(
                            y_ring[:, w, :].rearrange("p (h d) -> p h d", h=HEADS),
                            g_ring[:, v, :].rearrange("p (h d) -> p h d", h=HEADS), mv[:, 0, ds(cm, 1)],
                            rec_b[:, v, :][:, :, None].to_broadcast([P, HEADS, DH]), ALU.subtract, ALU.mult)\
                            .then_inc(s_msg, 1)
                    cr = c - 3
                    if exists(cr, EC):
                        w = (u - 3) % 2
                        dve.wait_ge(s_sum, cr + 1)
                        dve.wait_ge(s_masks, cr + 1)
                        at_least(dve, s_wag, cr - 1)
                        at_least(dve, s_run, cr)
                        if isinstance(cr, int) and cr == 0:
                            last = V.tensor_copy(y_ring[:, 2 + w, :], pair(w))
                        else:
                            for i in range(NC):
                                last = V.scalar_tensor_tensor(
                                    y_ring[:, 2 + w, i * P:(i + 1) * P], cont_m[:, w, :],
                                    y_ring[:, 3 - w, (i + 1) * P - 1:(i + 1) * P],
                                    pair(w)[:, i * P:(i + 1) * P], ALU.mult, ALU.add)
                        last.then_inc(s_run, 1)
            dve.wait_ge(s_wag, EC)
            for u in range(RING):
                dve.wait_ge(d_agg[u], 16 * (EC // RING))
            for b in turns(dve, NT // U, 2):
                for u in range(U):
                    t = b * U + u
                    if exists(t - 5, NT):
                        v = (u - 5) % U
                        dve.wait_ge(s_sq2, t - 4)
                        V.tensor_scalar(ve2[:, v:v + 1], ssq2[:, v:v + 1], 1.0 / D, EPS, ALU.mult, ALU.add)\
                            .then_inc(s_ve2, 1)
                    if exists(t - 6, NT):
                        v = (u - 6) % U
                        dve.wait_ge(s_r2, t - 5)
                        V.tensor_tensor(nm2[:, v:v + 1], nmean2[:, v:v + 1], r2[:, v:v + 1], ALU.mult)\
                            .then_inc(s_nm2, 1)
                    th = t - 9
                    if exists(th, NT):
                        v = (u - 9) % 2
                        dve.wait_ge(s_hhi, th + 1)
                        at_least(dve, s_down, th - 1)
                        V.tensor_tensor(h_lo[0:HID, v, :], h_sb[:, v, :], h_hi[0:HID, v, :].bitcast(f32),
                                        ALU.subtract).then_inc(s_hlo, 1)
                    if exists(t - 1, NT):
                        v = (u - 1) % U
                        dve.wait_ge(s_r1, t)
                        V.scalar_tensor_tensor(nm1[:, v:v + 1], mv1[:, v, 0:1], -1.0, r1[:, v:v + 1],
                                               ALU.mult, ALU.mult).then_inc(s_nm1, 1)
                    td = t - 10
                    if exists(td, NT):
                        v = (u - 10) % U
                        s = v % (2 * PAIR)
                        dve.wait_ge(s_down, td + 1)
                        if s % PAIR == 0:
                            k = v // PAIR
                            turn = b - 1 if u >= 2 else b - 2
                            at_least(dve, d_out[s // PAIR], 16 * (2 * turn + k // 2))
                        V.tensor_tensor(o_buf[:, s, :], y_ring[:, v, :], pair(2), ALU.add).then_inc(s_o, 1)
                    if exists(t, NT):
                        j = u // PAIR
                        if u % PAIR == 0:
                            dve.wait_ge(d_x[j], 16 * b + 16)
                            dve.wait_ge(d_nr[j], 16 * b + 16)
                            at_least(dve, s_add, t - U + PAIR)
                            V.tensor_scalar(has[:, u:u + PAIR], nrow[:, u:u + PAIR], float(EP), None, ALU.is_lt)\
                                .then_inc(s_has, PAIR)
                        for h in range(2):
                            V.bn_stats(bn1[:, u % 2, h, :], x_ring[:, u, h * (D // 2):(h + 1) * (D // 2)])\
                                .then_inc(s_bn1, 1)
                    tr = t - 3
                    vr = (u - 3) % U
                    if exists(tr, NT):
                        if vr % PAIR == 0:
                            n = b + 1 if u >= 3 else b
                            dve.wait_ge(d_g[vr // PAIR], 32 * n)
                            dve.wait_ge(s_has, tr + PAIR)
                        dve.wait_ge(s_res, tr + 1)
                        at_least(dve, s_o, tr - U + 1)
                        V.scalar_tensor_tensor(y_ring[:, vr, :], g_ring[:, vr, :], has[:, vr:vr + 1], pair(1),
                                               ALU.mult, ALU.add).then_inc(s_add, 1)
                    if exists(t, NT):
                        dve.wait_ge(s_bn1, 2 * t + 2)
                        at_least(dve, s_nm1, t - U + 1)
                        settle(dve)
                        V.bn_aggr(mv1[:, u, :], bn1[:, u % 2, :, :].rearrange("p a b -> p (a b)")).then_inc(s_ag1, 1)
                    if exists(tr, NT):
                        dve.wait_ge(s_add, tr + 1)
                        V.scalar_tensor_tensor(y_ring[:, vr, :], y_ring[:, vr, :], 0.0, x_ring[:, vr, :],
                                               ALU.max, ALU.add, accum_out=sum2[:, vr:vr + 1]).then_inc(s_y, 1)
                    if exists(t, NT):
                        dve.wait_ge(s_ag1, t + 1)
                        V.tensor_scalar(ve1[:, u:u + 1], mv1[:, u, 1:2], EPS, None, ALU.add).then_inc(s_ve1, 1)
                    if exists(tr, NT):
                        dve.wait_ge(s_y, tr + 1)
                        V.tensor_scalar(nmean2[:, vr:vr + 1], sum2[:, vr:vr + 1], -1.0 / D, None, ALU.mult)\
                            .then_inc(s_mean2, 1)
                        if isinstance(tr, int) and tr < PAIR:
                            V.tensor_copy(cls_x[:, tr, :], y_ring[0:NCLS // PAIR, vr, :]).then_inc(s_clsx, 1)
            dve.wait_ge(s_chg, NEXP)
            for s in range(2):
                for i in range(NCLS):
                    a, c = PAIRS[i][s]
                    last = V.tensor_copy(hm[:, s, c, i:i + 1], hc[:, a, i:i + 1])
            last.then_inc(s_chm, 1)
            dve.wait_ge(s_cg, 1)
            link_up(V.tensor_tensor(lg[:], ps[0:NCLS, 1, 0:2 * NCLS].rearrange("p (i g) -> p i g", g=2),
                                    ident[0:NCLS, 0:NCLS][:, :, None].to_broadcast([NCLS, NCLS, 2]), ALU.mult))
            link_up(V.tensor_reduce(gt[:, 0:2], lg[:].rearrange("p i g -> p g i"), axis=AX.X, op=ALU.add))
            link_up(V.tensor_tensor(gt[:, 2:3], gt[:, 0:1], gt[:, 1:2], ALU.max))
            V.tensor_scalar(gt[:, 0:2], gt[:, 0:2], gt[:, 2:3], None, ALU.subtract).then_inc(s_cmax, 1)
            dve.wait_ge(s_cexp, 1)
            link_up(V.tensor_tensor(gt[:, 6:7], gt[:, 4:5], gt[:, 5:6], ALU.add))
            link_up(V.reciprocal(gt[:, 7:8], gt[:, 6:7]))
            link_up(V.tensor_scalar(gt[:, 4:6], gt[:, 4:6], gt[:, 7:8], None, ALU.mult))
            link_up(V.tensor_tensor(gt[:, 8:9], gt[:, 4:5], gt[:, 5:6], ALU.min))
            link_up(V.tensor_scalar(gt[:, 10:12], gt[:, 4:6], gt[:, 8:9], None, ALU.is_gt))
            link_up(V.tensor_tensor(gt[:, 10:12], gt[:, 10:12], gt[:, 4:6], ALU.mult))
            link_up(V.tensor_tensor(gt[:, 12:13], gt[:, 10:11], gt[:, 11:12], ALU.add))
            link_up(V.tensor_scalar(gt[:, 12:13], gt[:, 12:13], 1e-6, None, ALU.max))
            link_up(V.reciprocal(gt[:, 13:14], gt[:, 12:13]))
            link_up(V.tensor_scalar(gt[:, 14:16], gt[:, 10:12], gt[:, 13:14], None, ALU.mult))
            dve.wait_ge(s_cs, 1)
            dve.wait_ge(l_clsx, 16)
            link_up(V.scalar_tensor_tensor(co[:, 1, :], pair(1)[0:NCLS, :], gt[:, 14:15], co[:, 0, :],
                                           ALU.mult, ALU.add))
            V.scalar_tensor_tensor(co[:, 2, :], pair(2)[0:NCLS, :], gt[:, 15:16], co[:, 1, :],
                                   ALU.mult, ALU.add).then_inc(s_cout, 1)


def kernel(x, src, dst, L0_gnn_W, L0_gnn_attn_l, L0_gnn_attn_r, L0_gnn_W_res, L0_ffn_moe0_W1, L0_ffn_moe0_b1,
           L0_ffn_moe0_W2, L0_ffn_moe0_b2, L0_ffn_A1_W, L0_ffn_A1_b, L0_ffn_A2_W, L0_ffn_A2_b, L0_ffn_G_W,
           L0_ffn_mids):
    import concourse.bacc as bacc
    from concourse.bass_utils import run_bass_kernel_spmd

    def rows(a, n, fill):
        a = np.asarray(a)
        return np.concatenate([a, np.full((n - a.shape[0],) + a.shape[1:], fill, a.dtype)])

    def block_diagonal(w):
        out = np.zeros((P, P), w.dtype)
        for i in range(HC):
            out[i * DH:(i + 1) * DH, i * DH:(i + 1) * DH] = w.T
        return out

    src = rows(np.asarray(src, np.int32), EP, 0)
    dst = rows(np.asarray(dst, np.int32), EP, PAD_NODE)
    dst_next = np.concatenate([dst[1:], np.full(1, -1, np.int32)])
    edges = np.stack([src, dst, np.zeros(EP, np.int32), np.arange(EP, dtype=np.int32)], axis=1)
    w, w_res = np.asarray(L0_gnn_W), np.asarray(L0_gnn_W_res)
    attn = np.concatenate([np.asarray(L0_gnn_attn_l)[0].T, np.asarray(L0_gnn_attn_r)[0].T], axis=1)
    arrays = {
        "x": rows(x, NP, 0),
        "edges": edges.reshape(EC, P, 4).transpose(1, 0, 2),
        "dst_next": dst_next.reshape(EC, P).T,
        "dst_a": dst.reshape(P, EC),
        "dst_row": dst.reshape(1, EP),
        "dst_first": dst.reshape(P, EC)[:, 0].reshape(1, P),
        "dst_last": dst.reshape(P, EC)[:, EC - 1].reshape(1, P),
        "eye": np.eye(P, dtype=np.float32),
        "w_gnn": w,
        "w_gnn_bd": block_diagonal(w),
        "w_res_bd": block_diagonal(w_res),
        "attn": attn,
        "w1": L0_ffn_moe0_W1,
        "b1": L0_ffn_moe0_b1,
        "w2": L0_ffn_moe0_W2,
        "b2": L0_ffn_moe0_b2,
        "a1w": np.asarray(L0_ffn_A1_W).transpose(1, 0, 2),
        "a1b": np.asarray(L0_ffn_A1_b).T,
        "a2w": np.asarray(L0_ffn_A2_W).transpose(1, 0, 2),
        "a2b": L0_ffn_A2_b,
        "gw": np.asarray(L0_ffn_G_W).transpose(1, 0, 2).reshape(D, 2 * NCLS),
    }
    nc = bacc.Bacc("TRN2", target_bir_lowering=False, num_devices=1)
    sent, args = {}, []
    for name, a in arrays.items():
        a = np.ascontiguousarray(a)
        sent[f"in_{name}"] = a
        args.append(nc.dram_tensor(f"in_{name}", a.shape, mybir.dt.from_np(a.dtype), kind="ExternalInput").ap())
    args.append(nc.dram_tensor("out", (NP, D), mybir.dt.float32, kind="ExternalOutput").ap())
    gnn_ffn_kernel(nc, *args)
    r = run_bass_kernel_spmd(nc, [sent], core_ids=[0])
    return r.results[0]["out"][:N_NODES]
```
